# Optimizing a Trainium2 kernel written in Bass

```python
import numpy as np
import jax
import jax.numpy as jnp

def _softmax(x, axis=-1):
    return jax.nn.softmax(x, axis=axis)

def _gelu(x):
    return jax.nn.gelu(x, approximate=True)

def _silu(x):
    return jax.nn.silu(x)

def _sigmoid(x):
    return jax.nn.sigmoid(x)

def _layernorm(x, axis=-1, eps=1e-05):
    m = jnp.mean(x, axis=axis, keepdims=True)
    v = jnp.var(x, axis=axis, keepdims=True)
    return (x - m) / jnp.sqrt(v + eps)

def _scatter_add(tgt, idx, src, axis=0):
    return tgt.at[idx].add(src)

def _segment_sum(src, seg, n):
    return jax.ops.segment_sum(src, seg, n)
kernel_name = 'mk_adaln_ffn_d2_seqx_r8_c3b6b3'

def setup_inputs(seed: int=0):
    np.random.seed(seed)
    _w = jnp.asarray

    def _rec_inputs():
        import jax
        import jax.numpy as jnp
        _rk = jax.random.key(seed)
        x = 7.22e-05 + 1 * jax.random.normal(jax.random.fold_in(_rk, 1), (32, 32, 128), jnp.float32)
        _lenS = 32 - jax.random.randint(jax.random.fold_in(_rk, 7), (32,), 0, max(1, 32 // 4) + 1, jnp.int32)
        _lenS2 = 32 - jax.random.randint(jax.random.fold_in(_rk, 8), (32,), 0, max(1, 32 // 4) + 1, jnp.int32)
        cond_64 = -0.104238 + 1.01173 * jax.random.normal(jax.random.fold_in(_rk, 11), (32, 64), jnp.float32)
        _validS = jnp.arange(32)[None, :] < _lenS[:, None]
        _validS2 = jnp.arange(32)[None, :] < _lenS2[:, None]
        _causal = jnp.tril(jnp.ones((32, 32), dtype=bool))
        mask_BxS_bf1 = jnp.ones((32, 32), dtype=bool)
        return (x, cond_64, mask_BxS_bf1)
    x, cond_64, mask_BxS_bf1 = _rec_inputs()

    def _L0_cond_setup():
        import jax, jax.numpy as jnp
        import numpy as np
        B, S, H = (4, 256, 128)
        E = 8
        M = 64
        K = 2
        N_SHARED = 2
        SM = M * N_SHARED
        G = 64
        GE_TEMP = 1.0
        ALPHA = 0.001
        SEQ_AUX = True
        NORM_TOPK = True
        COS_TEMP = 0.78
        CONS_ALPHA = 0.01
        LEAKY_SLOPE = 0.01
        EPS_COS = 1e-08

        def _leaky(x):
            return jnp.where(x >= 0, x, LEAKY_SLOPE * x)

        def _moe_forward(hidden_states, g, wt, wg, w_gate, w_up, w_down, sw_gate, sw_up, sw_down):
            b, s, h = hidden_states.shape
            x = hidden_states.reshape(-1, h)
            T = x.shape[0]
            logits_h = x @ wt.T
            logits_g = g @ wg.T
            logits_g = jnp.repeat(logits_g, s, axis=0)
            logits = (logits_h + logits_g / GE_TEMP) / (1.0 + 1.0 / GE_TEMP)
            scores = jax.nn.softmax(logits, axis=-1)
            topk_w, topk_idx = jax.lax.top_k(scores, K)
            if K > 1 and NORM_TOPK:
                topk_w = topk_w / (topk_w.sum(-1, keepdims=True) + 1e-20)
            onehot = jax.nn.one_hot(topk_idx.reshape(b, s * K), E, dtype=jnp.float32)
            ce = onehot.sum(1) / (s * K / E)
            aux_loss = (ce * scores.reshape(b, s, E).mean(1)).sum(1).mean() * ALPHA
            gp = _leaky(jnp.einsum('th,ehm->etm', x, w_gate))
            up = jnp.einsum('th,ehm->etm', x, w_up)
            y_all = jnp.einsum('etm,emh->eth', gp * up, w_down)
            y_sel = y_all[topk_idx, jnp.arange(T)[:, None], :]
            y = (y_sel * topk_w[..., None]).sum(1).reshape(b, s, h)
            p = _leaky(hidden_states @ sw_gate) * (hidden_states @ sw_up) @ sw_down
            y = y + p
            num = jnp.sum(y * p, -1)
            den = jnp.maximum(jnp.linalg.norm(y, axis=-1), EPS_COS) * jnp.maximum(jnp.linalg.norm(p, axis=-1), EPS_COS)
            closs = CONS_ALPHA * jnp.mean(num / den / (1.0 + COS_TEMP))
            return (y, aux_loss + closs)
        key = jax.random.key(seed)
        ks = jax.random.split(key, 12)
        sh = 1.0 / np.sqrt(H)
        sm = 1.0 / np.sqrt(M)
        ssm = 1.0 / np.sqrt(SM)
        sg = 1.0 / np.sqrt(G)
        return {'hidden_states': jax.random.normal(ks[0], (B, S, H), jnp.float32), 'g': jax.random.normal(ks[1], (B, G), jnp.float32), 'wt': jax.random.uniform(ks[2], (E, H), jnp.float32, -sh, sh), 'wg': jax.random.uniform(ks[3], (E, G), jnp.float32, -sg, sg), 'w_gate': jax.random.uniform(ks[4], (E, H, M), jnp.float32, -sh, sh), 'w_up': jax.random.uniform(ks[5], (E, H, M), jnp.float32, -sh, sh), 'w_down': jax.random.uniform(ks[6], (E, M, H), jnp.float32, -sm, sm), 'sw_gate': jax.random.uniform(ks[7], (H, SM), jnp.float32, -sh, sh), 'sw_up': jax.random.uniform(ks[8], (H, SM), jnp.float32, -sh, sh), 'sw_down': jax.random.uniform(ks[9], (SM, H), jnp.float32, -ssm, ssm)}
    _L0_cond_all = _L0_cond_setup()
    _L0_cond_in = {k: v for k, v in _L0_cond_all.items() if k in ('wt', 'wg', 'w_gate', 'w_up', 'w_down', 'sw_gate', 'sw_up', 'sw_down')}
    del _L0_cond_all

    def _L0_ffn_setup():
        import jax, jax.numpy as jnp
        import numpy as np
        H = 128
        M = 64
        E = 16
        TOP_K = 4
        N_GROUP = 4
        TOPK_GROUP = 2
        SCALE = 2.5
        B, S = (2, 128)

        def _gate(x2d, gate_kernel, gate_bias):
            n = x2d.shape[0]
            logits = jnp.dot(x2d.astype(jnp.float32), gate_kernel.astype(jnp.float32))
            scores = jax.nn.sigmoid(logits)
            scores_for_choice = scores + gate_bias
            group_scores = scores_for_choice.reshape(n, N_GROUP, E // N_GROUP)
            top2 = jax.lax.top_k(group_scores, k=2)[0]
            group_sum = jnp.sum(top2, axis=-1)
            group_idx = jax.lax.top_k(group_sum, k=TOPK_GROUP)[1]
            group_mask = jnp.zeros_like(group_sum).at[jnp.arange(n)[:, None], group_idx].set(1.0)
            score_mask = jnp.repeat(group_mask[:, :, None], E // N_GROUP, axis=2).reshape(n, E)
            masked_scores = jnp.where(score_mask > 0, scores_for_choice, 0.0)
            topk_weight, topk_idx = jax.lax.top_k(masked_scores, k=TOP_K)
            topk_weight = topk_weight / (jnp.sum(topk_weight, axis=-1, keepdims=True) + 1e-20)
            topk_weight = topk_weight * SCALE
            return (topk_idx, topk_weight)
        key = jax.random.key(seed)
        ks = jax.random.split(key, 9)
        sc_h = 1.0 / np.sqrt(H)
        sc_m = 1.0 / np.sqrt(M)
        return {'hidden_states': jax.random.normal(ks[0], (B, S, H), jnp.float32), 'gate_kernel': jax.random.normal(ks[1], (H, E), jnp.float32) * sc_h, 'gate_bias': jax.random.normal(ks[2], (E,), jnp.float32) * 0.01, 'w_gate': jax.random.normal(ks[3], (E, H, M), jnp.float32) * sc_h, 'w_up': jax.random.normal(ks[4], (E, H, M), jnp.float32) * sc_h, 'w_down': jax.random.normal(ks[5], (E, M, H), jnp.float32) * sc_m, 'sw_gate': jax.random.normal(ks[6], (H, 2 * M), jnp.float32) * sc_h, 'sw_up': jax.random.normal(ks[7], (H, 2 * M), jnp.float32) * sc_h, 'sw_down': jax.random.normal(ks[8], (2 * M, H), jnp.float32) * (1.0 / np.sqrt(2 * M))}
    _L0_ffn_all = _L0_ffn_setup()
    _L0_ffn_in = {k: v for k, v in _L0_ffn_all.items() if k in ('gate_kernel', 'gate_bias', 'w_gate', 'w_up', 'w_down', 'sw_gate', 'sw_up', 'sw_down')}
    del _L0_ffn_all

    def _L1_cond_setup():
        import jax, jax.numpy as jnp
        import numpy as np
        DIM = 128
        HEADS = 16
        DIM_HEAD = 64
        SCALE = 8.0

        def ln(x, g, eps=1e-05):
            mean = x.mean(axis=-1, keepdims=True)
            var = ((x - mean) ** 2).mean(axis=-1, keepdims=True)
            return (x - mean) * jax.lax.rsqrt(var + eps) * g

        def l2norm(t):
            n = jnp.maximum(jnp.linalg.norm(t, axis=-1, keepdims=True), 1e-12)
            return t / n

        def rel_pos_bias(n, w0, b0, g0, w1, b1, g1, w2, b2, dtype):
            pos = jnp.arange(-n + 1, n, dtype=dtype)[:, None]
            h = jax.nn.silu(ln(pos @ w0 + b0, g0))
            h = jax.nn.silu(ln(h @ w1 + b1, g1))
            h = h @ w2 + b2
            i = jnp.arange(n)
            idx = i[:, None] - i[None, :] + n - 1
            bias = h[idx]
            return jnp.transpose(bias, (2, 0, 1))
        key = jax.random.key(seed)
        ks = jax.random.split(key, 16)
        b, n = (2, 256)
        inner = HEADS * DIM_HEAD
        s = 0.02
        return {'x': jax.random.normal(ks[0], (b, n, DIM), jnp.float32), 'mask': jnp.ones((b, n), dtype=bool), 'g_norm': jnp.ones((DIM,), jnp.float32), 'Wq': jax.random.normal(ks[1], (DIM, inner), jnp.float32) * s, 'Wkv': jax.random.normal(ks[2], (DIM, 2 * DIM_HEAD), jnp.float32) * s, 'q_scale': jnp.ones((DIM_HEAD,), jnp.float32), 'k_scale': jnp.ones((DIM_HEAD,), jnp.float32), 'null_kv': jax.random.normal(ks[3], (2, DIM_HEAD), jnp.float32), 'null_attn_bias': jax.random.normal(ks[4], (HEADS,), jnp.float32), 'w0': jax.random.normal(ks[5], (1, DIM), jnp.float32) * s, 'b0': jnp.zeros((DIM,), jnp.float32), 'g0': jnp.ones((DIM,), jnp.float32), 'w1': jax.random.normal(ks[6], (DIM, DIM), jnp.float32) * s, 'b1': jnp.zeros((DIM,), jnp.float32), 'g1': jnp.ones((DIM,), jnp.float32), 'w2': jax.random.normal(ks[7], (DIM, HEADS), jnp.float32) * s, 'b2': jnp.zeros((HEADS,), jnp.float32), 'Wout': jax.random.normal(ks[8], (inner, DIM), jnp.float32) * s, 'g_out': jnp.ones((DIM,), jnp.float32)}
    _L1_cond_all = _L1_cond_setup()
    _L1_cond_in = {k: v for k, v in _L1_cond_all.items() if k in ('g_norm', 'Wq', 'Wkv', 'q_scale', 'k_scale', 'null_attn_bias', 'w0', 'b0', 'g0', 'w1', 'b1', 'g1', 'w2', 'b2', 'Wout', 'g_out')}
    del _L1_cond_all

    def _L1_ffn_setup():
        import jax, jax.numpy as jnp
        import numpy as np
        B, S, H, E, K = (2, 256, 128, 8, 2)
        FF = 4 * H
        EPS = 1e-05
        key = jax.random.key(seed)
        ks = jax.random.split(key, 5)
        rn = lambda k, shape, scale: jax.random.normal(k, shape, dtype=jnp.float32) * scale
        return {'x': rn(ks[0], (B, S, H), 1.0), 'router_W': rn(ks[1], (H, E), H ** (-0.5)), 'router_b': jnp.zeros((E,), jnp.float32), 'ln_g': jnp.ones((E, H), jnp.float32), 'ln_b': jnp.zeros((E, H), jnp.float32), 'W1': rn(ks[2], (E, H, FF), H ** (-0.5)), 'b1': jnp.zeros((E, FF), jnp.float32), 'W2': rn(ks[3], (E, FF, H), FF ** (-0.5)), 'b2': jnp.zeros((E, H), jnp.float32)}
    _L1_ffn_all = _L1_ffn_setup()
    _L1_ffn_in = {k: v for k, v in _L1_ffn_all.items() if k in ('router_W', 'router_b', 'ln_g', 'ln_b', 'W1', 'b1', 'W2', 'b2')}
    del _L1_ffn_all
    return {'x': x, 'cond_64': cond_64, 'mask_BxS_bf1': mask_BxS_bf1, 'L0_cond_wt': _L0_cond_in['wt'], 'L0_cond_wg': _L0_cond_in['wg'], 'L0_cond_w_gate': _L0_cond_in['w_gate'], 'L0_cond_w_up': _L0_cond_in['w_up'], 'L0_cond_w_down': _L0_cond_in['w_down'], 'L0_cond_sw_gate': _L0_cond_in['sw_gate'], 'L0_cond_sw_up': _L0_cond_in['sw_up'], 'L0_cond_sw_down': _L0_cond_in['sw_down'], 'L0_ffn_gate_kernel': _L0_ffn_in['gate_kernel'], 'L0_ffn_gate_bias': _L0_ffn_in['gate_bias'], 'L0_ffn_w_gate': _L0_ffn_in['w_gate'], 'L0_ffn_w_up': _L0_ffn_in['w_up'], 'L0_ffn_w_down': _L0_ffn_in['w_down'], 'L0_ffn_sw_gate': _L0_ffn_in['sw_gate'], 'L0_ffn_sw_up': _L0_ffn_in['sw_up'], 'L0_ffn_sw_down': _L0_ffn_in['sw_down'], 'L1_cond_g_norm': _L1_cond_in['g_norm'], 'L1_cond_Wq': _L1_cond_in['Wq'], 'L1_cond_Wkv': _L1_cond_in['Wkv'], 'L1_cond_q_scale': _L1_cond_in['q_scale'], 'L1_cond_k_scale': _L1_cond_in['k_scale'], 'L1_cond_null_attn_bias': _L1_cond_in['null_attn_bias'], 'L1_cond_w0': _L1_cond_in['w0'], 'L1_cond_b0': _L1_cond_in['b0'], 'L1_cond_g0': _L1_cond_in['g0'], 'L1_cond_w1': _L1_cond_in['w1'], 'L1_cond_b1': _L1_cond_in['b1'], 'L1_cond_g1': _L1_cond_in['g1'], 'L1_cond_w2': _L1_cond_in['w2'], 'L1_cond_b2': _L1_cond_in['b2'], 'L1_cond_Wout': _L1_cond_in['Wout'], 'L1_cond_g_out': _L1_cond_in['g_out'], 'L1_ffn_router_W': _L1_ffn_in['router_W'], 'L1_ffn_router_b': _L1_ffn_in['router_b'], 'L1_ffn_ln_g': _L1_ffn_in['ln_g'], 'L1_ffn_ln_b': _L1_ffn_in['ln_b'], 'L1_ffn_W1': _L1_ffn_in['W1'], 'L1_ffn_b1': _L1_ffn_in['b1'], 'L1_ffn_W2': _L1_ffn_in['W2'], 'L1_ffn_b2': _L1_ffn_in['b2']}

def reference(x, cond_64, mask_BxS_bf1, L0_cond_wt, L0_cond_wg, L0_cond_w_gate, L0_cond_w_up, L0_cond_w_down, L0_cond_sw_gate, L0_cond_sw_up, L0_cond_sw_down, L0_ffn_gate_kernel, L0_ffn_gate_bias, L0_ffn_w_gate, L0_ffn_w_up, L0_ffn_w_down, L0_ffn_sw_gate, L0_ffn_sw_up, L0_ffn_sw_down, L1_cond_g_norm, L1_cond_Wq, L1_cond_Wkv, L1_cond_q_scale, L1_cond_k_scale, L1_cond_null_attn_bias, L1_cond_w0, L1_cond_b0, L1_cond_g0, L1_cond_w1, L1_cond_b1, L1_cond_g1, L1_cond_w2, L1_cond_b2, L1_cond_Wout, L1_cond_g_out, L1_ffn_router_W, L1_ffn_router_b, L1_ffn_ln_g, L1_ffn_ln_b, L1_ffn_W1, L1_ffn_b1, L1_ffn_W2, L1_ffn_b2):
    import jax
    import jax.numpy as jnp

    def _L0_cond_ref(hidden_states, g, wt, wg, w_gate, w_up, w_down, sw_gate, sw_up, sw_down):
        import jax, jax.numpy as jnp
        import numpy as np
        B, S, H = (4, 256, 128)
        E = 8
        M = 64
        K = 2
        N_SHARED = 2
        SM = M * N_SHARED
        G = 64
        GE_TEMP = 1.0
        ALPHA = 0.001
        SEQ_AUX = True
        NORM_TOPK = True
        COS_TEMP = 0.78
        CONS_ALPHA = 0.01
        LEAKY_SLOPE = 0.01
        EPS_COS = 1e-08

        def _leaky(x):
            return jnp.where(x >= 0, x, LEAKY_SLOPE * x)

        def _moe_forward(hidden_states, g, wt, wg, w_gate, w_up, w_down, sw_gate, sw_up, sw_down):
            b, s, h = hidden_states.shape
            x = hidden_states.reshape(-1, h)
            T = x.shape[0]
            logits_h = x @ wt.T
            logits_g = g @ wg.T
            logits_g = jnp.repeat(logits_g, s, axis=0)
            logits = (logits_h + logits_g / GE_TEMP) / (1.0 + 1.0 / GE_TEMP)
            scores = jax.nn.softmax(logits, axis=-1)
            topk_w, topk_idx = jax.lax.top_k(scores, K)
            if K > 1 and NORM_TOPK:
                topk_w = topk_w / (topk_w.sum(-1, keepdims=True) + 1e-20)
            onehot = jax.nn.one_hot(topk_idx.reshape(b, s * K), E, dtype=jnp.float32)
            ce = onehot.sum(1) / (s * K / E)
            aux_loss = (ce * scores.reshape(b, s, E).mean(1)).sum(1).mean() * ALPHA
            gp = _leaky(jnp.einsum('th,ehm->etm', x, w_gate))
            up = jnp.einsum('th,ehm->etm', x, w_up)
            y_all = jnp.einsum('etm,emh->eth', gp * up, w_down)
            y_sel = y_all[topk_idx, jnp.arange(T)[:, None], :]
            y = (y_sel * topk_w[..., None]).sum(1).reshape(b, s, h)
            p = _leaky(hidden_states @ sw_gate) * (hidden_states @ sw_up) @ sw_down
            y = y + p
            num = jnp.sum(y * p, -1)
            den = jnp.maximum(jnp.linalg.norm(y, axis=-1), EPS_COS) * jnp.maximum(jnp.linalg.norm(p, axis=-1), EPS_COS)
            closs = CONS_ALPHA * jnp.mean(num / den / (1.0 + COS_TEMP))
            return (y, aux_loss + closs)
        y, _ = _moe_forward(hidden_states, g, wt, wg, w_gate, w_up, w_down, sw_gate, sw_up, sw_down)
        return y

    def _L0_ffn_ref(hidden_states, gate_kernel, gate_bias, w_gate, w_up, w_down, sw_gate, sw_up, sw_down):
        import jax, jax.numpy as jnp
        import numpy as np
        H = 128
        M = 64
        E = 16
        TOP_K = 4
        N_GROUP = 4
        TOPK_GROUP = 2
        SCALE = 2.5
        B, S = (2, 128)

        def _gate(x2d, gate_kernel, gate_bias):
            n = x2d.shape[0]
            logits = jnp.dot(x2d.astype(jnp.float32), gate_kernel.astype(jnp.float32))
            scores = jax.nn.sigmoid(logits)
            scores_for_choice = scores + gate_bias
            group_scores = scores_for_choice.reshape(n, N_GROUP, E // N_GROUP)
            top2 = jax.lax.top_k(group_scores, k=2)[0]
            group_sum = jnp.sum(top2, axis=-1)
            group_idx = jax.lax.top_k(group_sum, k=TOPK_GROUP)[1]
            group_mask = jnp.zeros_like(group_sum).at[jnp.arange(n)[:, None], group_idx].set(1.0)
            score_mask = jnp.repeat(group_mask[:, :, None], E // N_GROUP, axis=2).reshape(n, E)
            masked_scores = jnp.where(score_mask > 0, scores_for_choice, 0.0)
            topk_weight, topk_idx = jax.lax.top_k(masked_scores, k=TOP_K)
            topk_weight = topk_weight / (jnp.sum(topk_weight, axis=-1, keepdims=True) + 1e-20)
            topk_weight = topk_weight * SCALE
            return (topk_idx, topk_weight)
        orig_shape = hidden_states.shape
        x = hidden_states.reshape(-1, orig_shape[-1])
        topk_idx, topk_weight = _gate(x, gate_kernel, gate_bias)
        onehot = (topk_idx[:, :, None] == jnp.arange(E)[None, None, :]).astype(topk_weight.dtype)
        combine = jnp.einsum('nke,nk->ne', onehot, topk_weight)
        g = jnp.einsum('nh,ehm->enm', x, w_gate)
        u = jnp.einsum('nh,ehm->enm', x, w_up)
        inter = jax.nn.silu(g) * u
        y_e = jnp.einsum('enm,emh->enh', inter, w_down)
        y = jnp.einsum('ne,enh->nh', combine, y_e)
        shared = jnp.dot(jax.nn.silu(jnp.dot(x, sw_gate)) * jnp.dot(x, sw_up), sw_down)
        return (y + shared).reshape(orig_shape)

    def _L1_cond_ref(x, mask, g_norm, Wq, Wkv, q_scale, k_scale, null_kv, null_attn_bias, w0, b0, g0, w1, b1, g1, w2, b2, Wout, g_out):
        import jax, jax.numpy as jnp
        import numpy as np
        DIM = 128
        HEADS = 16
        DIM_HEAD = 64
        SCALE = 8.0

        def ln(x, g, eps=1e-05):
            mean = x.mean(axis=-1, keepdims=True)
            var = ((x - mean) ** 2).mean(axis=-1, keepdims=True)
            return (x - mean) * jax.lax.rsqrt(var + eps) * g

        def l2norm(t):
            n = jnp.maximum(jnp.linalg.norm(t, axis=-1, keepdims=True), 1e-12)
            return t / n

        def rel_pos_bias(n, w0, b0, g0, w1, b1, g1, w2, b2, dtype):
            pos = jnp.arange(-n + 1, n, dtype=dtype)[:, None]
            h = jax.nn.silu(ln(pos @ w0 + b0, g0))
            h = jax.nn.silu(ln(h @ w1 + b1, g1))
            h = h @ w2 + b2
            i = jnp.arange(n)
            idx = i[:, None] - i[None, :] + n - 1
            bias = h[idx]
            return jnp.transpose(bias, (2, 0, 1))
        b, n, _ = x.shape
        xn = ln(x, g_norm)
        q = (xn @ Wq).reshape(b, n, HEADS, DIM_HEAD).transpose(0, 2, 1, 3)
        kv = xn @ Wkv
        k, v = (kv[..., :DIM_HEAD], kv[..., DIM_HEAD:])
        nk = jnp.broadcast_to(null_kv[0], (b, 1, DIM_HEAD))
        nv = jnp.broadcast_to(null_kv[1], (b, 1, DIM_HEAD))
        k = jnp.concatenate([nk, k], axis=1)
        v = jnp.concatenate([nv, v], axis=1)
        q = l2norm(q) * q_scale
        k = l2norm(k) * k_scale
        sim = jnp.einsum('bhid,bjd->bhij', q, k) * SCALE
        bias = rel_pos_bias(n, w0, b0, g0, w1, b1, g1, w2, b2, q.dtype)
        null_bias = jnp.broadcast_to(null_attn_bias[:, None, None], (HEADS, n, 1))
        attn_bias = jnp.concatenate([null_bias, bias], axis=-1)
        sim = sim + attn_bias
        neg = -jnp.finfo(sim.dtype).max
        causal = jnp.triu(jnp.ones((n, n + 1), dtype=bool), k=2)
        sim = jnp.where(causal, neg, sim)
        m = jnp.pad(mask, ((0, 0), (1, 0)), constant_values=True)[:, None, None, :]
        sim = jnp.where(m, sim, neg)
        attn = jax.nn.softmax(sim, axis=-1)
        out = jnp.einsum('bhij,bjd->bhid', attn, v)
        out = out.transpose(0, 2, 1, 3).reshape(b, n, HEADS * DIM_HEAD)
        return ln(out @ Wout, g_out)

    def _L1_ffn_ref(x, router_W, router_b, ln_g, ln_b, W1, b1, W2, b2):
        import jax, jax.numpy as jnp
        import numpy as np
        B, S, H, E, K = (2, 256, 128, 8, 2)
        FF = 4 * H
        EPS = 1e-05
        logits = x @ router_W + router_b
        w, idx = jax.lax.top_k(logits, K)
        w = jax.nn.softmax(w, axis=-1)
        gates = jnp.einsum('bske,bsk->bse', jax.nn.one_hot(idx, E, dtype=x.dtype), w)
        mu = jnp.mean(x, axis=-1, keepdims=True)
        var = jnp.mean(jnp.square(x - mu), axis=-1, keepdims=True)
        xhat = (x - mu) * jax.lax.rsqrt(var + EPS)
        h = xhat[:, :, None, :] * ln_g + ln_b
        a = jax.nn.gelu(jnp.einsum('bseh,ehf->bsef', h, W1) + b1, approximate=False)
        y = jnp.einsum('bsef,efh->bseh', a, W2) + b2
        y = y + x[:, :, None, :]
        out = jnp.einsum('bseh,bse->bsh', y, gates)
        return out
    x = x + _L0_ffn_ref(_L0_cond_ref(x, cond_64, L0_cond_wt, L0_cond_wg, L0_cond_w_gate, L0_cond_w_up, L0_cond_w_down, L0_cond_sw_gate, L0_cond_sw_up, L0_cond_sw_down), L0_ffn_gate_kernel, L0_ffn_gate_bias, L0_ffn_w_gate, L0_ffn_w_up, L0_ffn_w_down, L0_ffn_sw_gate, L0_ffn_sw_up, L0_ffn_sw_down)
    x = x + _L1_ffn_ref(_L1_cond_ref(x, mask_BxS_bf1, L1_cond_g_norm, L1_cond_Wq, L1_cond_Wkv, L1_cond_q_scale, L1_cond_k_scale, cond_64, L1_cond_null_attn_bias, L1_cond_w0, L1_cond_b0, L1_cond_g0, L1_cond_w1, L1_cond_b1, L1_cond_g1, L1_cond_w2, L1_cond_b2, L1_cond_Wout, L1_cond_g_out), L1_ffn_router_W, L1_ffn_router_b, L1_ffn_ln_g, L1_ffn_ln_b, L1_ffn_W1, L1_ffn_b1, L1_ffn_W2, L1_ffn_b2)
    return x

_drawn_inputs = setup_inputs


def setup_inputs(seed=0):
    import zlib

    import numpy as np

    out = dict(_drawn_inputs(seed))
    spreads = {'L1_cond_g_norm': (1.0, 0.2),
     'L1_cond_q_scale': (1.0, 0.2),
     'L1_cond_k_scale': (1.0, 0.2),
     'L1_cond_b0': (0.0, 0.1),
     'L1_cond_g0': (1.0, 0.2),
     'L1_cond_b1': (0.0, 0.1),
     'L1_cond_g1': (1.0, 0.541),
     'L1_cond_b2': (0.0, 0.1),
     'L1_cond_g_out': (1.0, 0.2),
     'L1_ffn_router_b': (0.0, 0.1),
     'L1_ffn_ln_g': (1.0, 0.2),
     'L1_ffn_ln_b': (0.0, 0.1),
     'L1_ffn_b1': (0.0, 0.1),
     'L1_ffn_b2': (0.0, 0.1)}
    factors = {'L0_ffn_gate_bias': 2.755}
    for name, (base, spread) in spreads.items():
        noise = np.random.default_rng([zlib.crc32(name.encode()), seed]).standard_normal(out[name].shape)
        drawn = base * np.exp(spread * noise) if base else spread * noise
        out[name] = jnp.asarray(drawn.astype(out[name].dtype))
    for name, factor in factors.items():
        out[name] = (out[name] * factor).astype(out[name].dtype)
    return out
```

```python
import concourse.bass as bass
from concourse import mybir
from contextlib import ExitStack

f32 = mybir.dt.float32
f32r = mybir.dt.float32r
i32 = mybir.dt.int32
u32 = mybir.dt.uint32
u8 = mybir.dt.uint8
ALU = mybir.AluOpType
ACT = mybir.ActivationFunctionType
AX = mybir.AxisListType.X

P = 128
SEQ, LEN = 32, 32
TOK = SEQ * LEN
TILES = TOK // P
HALVES = 2
HT = TILES // HALVES
HW = HT * P
BPT = P // LEN

C_EXP, C_PAIRS = 8, 4
C_BLK = C_PAIRS + 1
F_EXP, F_PAIRS = 16, 8
F_BLK = F_PAIRS + 1
F_GROUPS, F_TOPK, F_SCALE = 4, 4, 2.5
HEADS, DH = 16, 64
HB = HEADS // 2
KEYS = LEN + 1
M_EXP, M_FF = 8, 512
M_BLK = M_FF // P
POSN = 2 * LEN - 1
ATT_SCALE = 8.0
MASKED = -1e30
LN_EPS = 1e-5
NORM_EPS = 1e-12
TINY = 2e-38

C0, F0, Q0 = 0, 2 * C_BLK * P, 2 * C_BLK * P + 2 * F_BLK * P
WCOLS = Q0 + HEADS * DH
V_LNG, V_LNB, V_B1, V_B2, V_GN = 0, 8, 16, 48, 56
V_ROWS = 57


def two_layers(nc, a, out):
    comb_c_dram = nc.dram_tensor("comb_c", [C_EXP, TOK], f32, kind="Internal").ap()
    comb_f_dram = nc.dram_tensor("comb_f", [F_EXP, TOK], f32, kind="Internal").ap()
    gate_m_dram = nc.dram_tensor("gate_m", [M_EXP, TOK], f32, kind="Internal").ap()
    bias_dram = nc.dram_tensor("rel_bias", [HEADS, LEN, LEN], f32, kind="Internal").ap()

    ctx = ExitStack()
    with ctx:
        def sb(name, shape, dt=f32):
            return ctx.enter_context(nc.sbuf_tensor(name, shape, dt))

        def sem(name):
            return ctx.enter_context(nc.semaphore(name))

        x_tok = sb("x_tok", [P, TILES, P])
        xc = sb("xc", [P, TILES, P])
        act_T = sb("act_T", [P, TOK])
        act_hi = sb("act_hi", [P, TOK], f32r)
        act_lo = sb("act_lo", [P, TOK], f32r)
        w_stage = sb("w_stage", [P, WCOLS])
        w_hi = sb("w_hi", [P, WCOLS], f32r)
        w_lo = sb("w_lo", [P, WCOLS], f32r)
        c_down = sb("c_down", [P, C_BLK, P])
        f_down = sb("f_down", [P, F_BLK, P])
        w_out = sb("w_out", [P, HB, P])
        w_kv = sb("w_kv", [P, 2 * DH])
        arena1 = sb("arena1", [P, 9216])
        arena2 = sb("arena2", [P, 8192])
        att_bias = sb("att_bias", [P, TILES, HEADS, KEYS])
        base_bias = sb("base_bias", [P, HEADS, LEN])
        v_diag = sb("v_diag", [P, TILES, BPT, DH])
        k_diag = sb("k_diag", [P, SEQ, 2, KEYS])
        ident = sb("ident", [P, P])
        vec_rows = sb("vec_rows", [V_ROWS, P])
        vec = sb("vec", [P, V_ROWS])
        small_rows = sb("small_rows", [SEQ + C_EXP, DH])
        wt_rows = sb("wt_rows", [C_EXP, P])
        wt_T = sb("wt_T", [P, C_EXP])
        wg_T = sb("wg_T", [P, C_EXP])
        gk = sb("gk", [P, F_EXP])
        router_w = sb("router_w", [P, M_EXP])
        router_b = sb("router_b", [P, M_EXP])
        f_bias = sb("f_bias", [P, F_EXP])
        rp_w1 = sb("rp_w1", [P, P])
        rp_w2 = sb("rp_w2", [P, HEADS])
        rp_b2 = sb("rp_b2", [HEADS, 1])
        rp_T = sb("rp_T", [P, 2, POSN])
        rp_out = sb("rp_out", [HEADS, POSN])
        pos_i = sb("pos_i", [POSN, 1], i32)
        pos = sb("pos", [POSN, 1])
        g_out = sb("g_out", [P, P])
        qk_scale = sb("qk_scale", [P, 2, DH])
        s_dup = sb("s_dup", [P, DH])
        null_b = sb("null_b", [P, HEADS])
        nv_col = sb("nv_col", [P, 1])
        nv_sel = sb("nv_sel", [P, HB, HEADS])
        nv_out = sb("nv_out", [P, P])
        pn_T = sb("pn_T", [P, P])
        mask_u8 = sb("mask_u8", [P, TILES, LEN], u8)
        mask_add = sb("mask_add", [P, TILES, LEN])
        ahead8 = sb("ahead8", [P, 8, 8])
        ahead4 = sb("ahead4", [P, 4, 4])
        iota_i = sb("iota_i", [P, F_EXP], i32)
        iota16 = sb("iota16", [P, F_EXP])
        eps = sb("eps", [P, 1])
        r_z = sb("r_z", [P, TILES, 16])
        r_s = sb("r_s", [P, TILES, 16])
        r_m = sb("r_m", [P, TILES, 16])
        r_big = sb("r_big", [P, 512])
        r_rank = sb("r_rank", [P, TILES, 16])
        r_a = sb("r_a", [P, 8, 4])
        r_b = sb("r_b", [P, 8, 4])
        r_c = sb("r_c", [P, 8, 4])
        r_d = sb("r_d", [P, 8, 4])
        r_max = sb("r_max", [P, TILES, 8])
        r_idx = sb("r_idx", [P, TILES, 8], u32)
        r_idf = sb("r_idf", [P, TILES, 8])
        r_sum = sb("r_sum", [P, TILES])
        r_inv = sb("r_inv", [P, TILES])
        comb = sb("comb", [P, P])
        comb_T = sb("comb_T", [P, P])
        st6 = sb("st6", [P, 2, HT, 6])
        mv = sb("mv", [P, TILES, 2])
        std = sb("std", [P, TILES])
        rstd = sb("rstd", [P, TILES])
        rp_mv = sb("rp_mv", [POSN, 2, 2])
        rp_st = sb("rp_st", [POSN, 6])
        rp_sd = sb("rp_sd", [POSN, 2])
        n2 = sb("n2", [P, TILES + 1, HEADS])
        rn = sb("rn", [P, TILES + 1, HEADS])
        k2sum = sb("k2sum", [P, TILES + 1])
        k2rn = sb("k2rn", [P, TILES + 1])
        smax = sb("smax", [P, 2, HEADS])
        ssum = sb("ssum", [P, 2, HEADS])
        p_null = sb("p_null", [P, 2, HEADS])
        g_sum = sb("g_sum", [P, TILES])

        g_sb = xc[:, :, :].rearrange("p t c -> p (t c)").rearrange("p (r t) -> p r t", r=2)
        g_lk = arena2[:, 1024:2048].rearrange("p (r t) -> p r t", r=2)
        early = att_bias[:, :, :, :].rearrange("p t h k -> p (t h k)")
        rp_rows = early[0:POSN, 0:5 * P].rearrange("p (n c) -> p n c", c=P)
        rp_h = early[0:POSN, 5 * P:7 * P].rearrange("p (n c) -> p n c", c=P)
        c_hid = arena1[:, 0:C_BLK * TOK].rearrange("p (b t) -> p b t", t=TOK)
        c_gate = arena1[:, C_BLK * TOK:(C_BLK + C_PAIRS) * TOK].rearrange("p (b t) -> p b t", t=TOK)
        f_hid = arena1[:, 0:F_BLK * TOK].rearrange("p (b t) -> p b t", t=TOK)
        q_T = arena1[:, 0:HB * TOK].rearrange("p (b t) -> p b t", t=TOK)
        gelu = arena1[:, 0:4096].rearrange("p (r b t) -> p r b t", r=2, b=M_BLK)
        x_exp = arena1[:, 4096:5120].rearrange("p (r t) -> p r t", r=2)
        y_tmp = arena1[:, 5120:6144].rearrange("p (r t) -> p r t", r=2)
        y_acc = arena1[:, 6144:7168].rearrange("p (s t) -> p s t", s=2)
        xh_tok = arena1[:, 7168:8192].rearrange("p (t c) -> p t c", c=P)
        f_gate = arena2[:, :].rearrange("p (b t) -> p b t", t=TOK)
        m_gate = arena2[:, :].rearrange("p (b t) -> p b t", t=TOK)
        g_tok_T = arena2[:, 0:TOK]
        xn_tok = arena2[:, 0:TOK].rearrange("p (t c) -> p t c", c=P)
        q_sq = arena2[:, 0:2048].rearrange("p (r c) -> p r c", r=2)
        q_hat = arena2[:, 2048:4096].rearrange("p (r c) -> p r c", r=2)
        k_tok = arena2[:, 4096:4672].rearrange("p (t d) -> p t d", d=DH)
        k_sq = arena2[:, 4672:5248].rearrange("p (t d) -> p t d", d=DH)
        k_dup = arena2[:, 5248:6400].rearrange("p (t u d) -> p t u d", u=2, d=DH)
        att_T = arena2[:, 0:2048].rearrange("p (r b t) -> p r b t", r=2, b=HB)
        s_buf = arena2[:, 2048:3104].rearrange("p (r h k) -> p r h k", r=2, h=HEADS)
        e_buf = arena2[:, 3104:4160].rearrange("p (r h k) -> p r h k", r=2, h=HEADS)
        p_buf = arena2[:, 4160:5184].rearrange("p (r h k) -> p r h k", r=2, h=HEADS)
        pT_buf = arena2[:, 5184:6208].rearrange("p (r h k) -> p r h k", r=2, h=HEADS)

        ps = ctx.enter_context(nc.psum_tensor("ps", [P, 8, 512], f32))

        def bank(n):
            return ps[:, n, :]

        def split_cols(base, blocks, b):
            return lambda w: w[:, base:base + 2 * blocks * P].rearrange(
                "p (g c) -> p g c", g=2)[:, :, b * P:(b + 1) * P]

        chunks = [split_cols(C0, C_BLK, b) for b in range(C_BLK)]
        chunks += [split_cols(F0, F_BLK, b) for b in range(F_BLK)]
        chunks += [(lambda w, j=j: w[:, Q0 + j * HW:Q0 + (j + 1) * HW]) for j in range(2)]
        CH_F, CH_Q, CH_N = C_BLK, C_BLK + F_BLK, C_BLK + F_BLK + 2

        ld = {n: sem("ld_" + n) for n in (
            "x", "small", "vec", "wc", "wf", "wq", "cd", "fd", "wo", "kv", "gk", "rp", "att", "null",
            "comb_c", "gate_c", "comb_f", "gate_f0", "gate_f1", "bias_w", "bias_r", "w1", "w2",
            "gate_mw", "out")}
        m_gate_in = [sem(f"ld_gate_m{e}") for e in range(M_EXP)]
        ready = sem("pool_ready")
        pool_lo = sem("pool_lo")
        pool_mul = sem("pool_mul")
        pool_w1 = sem("pool_w1")
        pool_xe = sem("pool_xe")
        pool_acc = sem("pool_acc")
        pool_sub = sem("pool_sub")
        pool_prob = sem("pool_prob")
        pool_bias = sem("pool_bias")
        pool_chain = sem("pool_chain")
        act_chunk = sem("act_chunk")
        act_hi_s = sem("act_hi_s")
        act_exp = sem("act_exp")
        act_g = sem("act_g")
        act_rp = sem("act_rp")
        act_sqrt = sem("act_sqrt")
        act_sq = sem("act_sq")
        act_qT = sem("act_qT")
        act_pexp = sem("act_pexp")
        act_attT = sem("act_attT")
        act_w1 = sem("act_w1")
        act_xe = sem("act_xe")
        act_gelu = sem("act_gelu")
        pe_small = sem("pe_small")
        pe_xT = sem("pe_xT")
        pe_log = sem("pe_log")
        pe_up = sem("pe_up")
        pe_comb = sem("pe_comb")
        pe_down = sem("pe_down")
        pe_rp = sem("pe_rp")
        pe_kv = sem("pe_kv")
        pe_kT = sem("pe_kT")
        pe_q = sem("pe_q")
        pe_qT = sem("pe_qT")
        pe_sim = sem("pe_sim")
        pe_pn = sem("pe_pn")
        pe_av = sem("pe_av")
        pe_wo = sem("pe_wo")
        pe_nv = sem("pe_nv")
        pe_m_up = sem("pe_m_up")
        pe_m_down = sem("pe_m_down")
        pe_fin = sem("pe_fin")
        v_small = sem("v_small")
        v_T = sem("v_T")
        v_lo = sem("v_lo")
        v_z = sem("v_z")
        v_comb = sem("v_comb")
        v_combT = sem("v_combT")
        v_hid = sem("v_hid")
        v_mul = sem("v_mul")
        v_rp = sem("v_rp")
        v_var = sem("v_var")
        v_xn = sem("v_xn")
        v_k = sem("v_k")
        v_kv = sem("v_kv")
        v_kd = sem("v_kd")
        v_nv = sem("v_nv")
        v_n2 = sem("v_n2")
        v_red = sem("v_red")
        v_qhat = sem("v_qhat")
        v_bias = sem("v_bias")
        v_max = sem("v_max")
        v_rs = sem("v_rs")
        v_pT = sem("v_pT")
        v_pn = sem("v_pn")
        v_wo = sem("v_wo")
        v_y = sem("v_y")
        v_out = sem("v_out")
        v_chain = sem("v_chain")

        block = ctx.enter_context(nc.Block())

        @block.sync
        def _(sp):
            for s in range(HALVES):
                sp.dma_start(x_tok[:, s * HT:(s + 1) * HT, :],
                             a["x"].rearrange("b s c -> (b s) c").rearrange("(t p) c -> p t c", p=P)
                             [:, s * HT:(s + 1) * HT, :]).then_inc(ld["x"], 16)
            cview = w_stage[:, C0:C0 + 2 * C_BLK * P].rearrange("p (g c) -> p g c", g=2)
            fview = w_stage[:, F0:F0 + 2 * F_BLK * P].rearrange("p (g c) -> p g c", g=2)
            for view, pre, n, s in ((cview, "L0_cond_", C_PAIRS, "wc"), (fview, "L0_ffn_", F_PAIRS, "wf")):
                for g, name in enumerate(("gate", "up")):
                    sp.dma_start(view[:, g, 0:n * P].rearrange("p (e m) -> p e m", m=DH),
                                 a[pre + "w_" + name].rearrange("e h m -> h e m")).then_inc(ld[s], 16)
                    sp.dma_start(view[:, g, n * P:(n + 1) * P], a[pre + "sw_" + name]).then_inc(ld[s], 16)
            sp.dma_start(c_down[:, 0:C_PAIRS, :], a["L0_cond_w_down"].rearrange("(q e) m c -> (e m) q c", e=2))\
                .then_inc(ld["cd"], 16)
            sp.dma_start(c_down[:, C_PAIRS, :], a["L0_cond_sw_down"]).then_inc(ld["cd"], 16)
            sp.dma_start(w_stage[:, Q0:WCOLS], a["L1_cond_Wq"]).then_inc(ld["wq"], 16)
            sp.dma_start(f_down[:, 0:F_PAIRS, :], a["L0_ffn_w_down"].rearrange("(q e) m c -> (e m) q c", e=2))\
                .then_inc(ld["fd"], 16)
            sp.dma_start(f_down[:, F_PAIRS, :], a["L0_ffn_sw_down"]).then_inc(ld["fd"], 16)
            sp.dma_start(w_kv[:, :], a["L1_cond_Wkv"]).then_inc(ld["kv"], 16)
            sp.dma_start(w_out[:, :, :], a["L1_cond_Wout"].rearrange("(b p) c -> p b c", p=P))\
                .then_inc(ld["wo"], 16)
            sp.wait_ge(v_combT, 1)
            sp.dma_start(comb_c_dram.rearrange("e (t k) -> (e t) k", k=P), comb_T[0:C_EXP * TILES, :])\
                .then_inc(ld["comb_c"], 16)
            sp.wait_ge(ld["comb_c"], 16)
            for e in range(2):
                sp.dma_start(c_gate[e * DH:(e + 1) * DH, :, :],
                             comb_c_dram.rearrange("(q e) k -> e q k", e=2)[e].partition_broadcast(DH))\
                    .then_inc(ld["gate_c"], 16)
            sp.wait_ge(v_combT, 2)
            sp.dma_start(comb_f_dram.rearrange("e (t k) -> (e t) k", k=P), comb_T[:, :])\
                .then_inc(ld["comb_f"], 16)
            sp.wait_ge(ld["comb_f"], 16)
            for s in range(HALVES):
                for e in range(2):
                    sp.dma_start(f_gate[e * DH:(e + 1) * DH, :, s * HW:(s + 1) * HW],
                                 comb_f_dram.rearrange("(q e) k -> e q k", e=2)[e, :, s * HW:(s + 1) * HW]
                                 .partition_broadcast(DH)).then_inc(ld[f"gate_f{s}"], 16)
            sp.wait_ge(v_rp, 8)
            row = rp_out[:, 0:LEN]
            skew = bass.AP(row.tensor, row.offset + LEN - 1, [list(row.ap[0]), [-1, LEN], [1, LEN]])
            sp.dma_start(bias_dram, skew).then_inc(ld["bias_w"], 16)
            sp.wait_ge(ld["bias_w"], 16)
            for s in range(BPT):
                sp.dma_start(base_bias[s * LEN:(s + 1) * LEN, :, :], bias_dram.rearrange("h i j -> i h j")).then_inc(ld["bias_r"], 16)
            sp.wait_ge(pool_lo, CH_N)
            sp.wait_ge(act_chunk, CH_N)
            w1_stage = w_stage[:, 0:M_EXP * M_FF].rearrange("p (e f) -> p e f", f=M_FF)
            sp.dma_start(w1_stage, a["L1_ffn_W1"].rearrange("e h f -> h e f")).then_inc(ld["w1"], 16)
            sp.wait_ge(pe_down, 4)
            sp.dma_start(k_tok[:, TILES, :], a["cond_64"][0, :].partition_broadcast(P)).then_inc(ld["null"], 16)
            sp.wait_ge(pool_w1, M_EXP)
            sp.wait_ge(act_w1, M_EXP)
            w2_stage = w_stage[:, 0:M_EXP * M_FF].rearrange("p (e b c) -> p e b c", e=M_EXP, c=P)
            for e in range(M_EXP):
                sp.dma_start(w2_stage[:, e], a["L1_ffn_W2"][e].rearrange("(b p) c -> p b c", p=P))\
                    .then_inc(ld["w2"], 16)
            sp.wait_ge(v_combT, 3)
            sp.dma_start(gate_m_dram.rearrange("e (t k) -> (e t) k", k=P), comb_T[0:M_EXP * TILES, :])\
                .then_inc(ld["gate_mw"], 16)
            sp.wait_ge(ld["gate_mw"], 16)
            for e in range(M_EXP):
                sp.dma_start(m_gate[:, e, :], gate_m_dram[e].partition_broadcast(P)).then_inc(m_gate_in[e], 16)
            for s in range(HALVES):
                sp.wait_ge(v_out, s + 1)
                sp.dma_start(out.rearrange("b s c -> (b s) c").rearrange("(t p) c -> p t c", p=P)
                             [:, s * HT:(s + 1) * HT, :], x_tok[:, s * HT:(s + 1) * HT, :])\
                    .then_inc(ld["out"], 16)
            sp.wait_ge(ld["out"], 32)

        @block.gpsimd
        def _(pool):
            n_chain = [0]

            def link(ins):
                n_chain[0] += 1
                ins.then_inc(pool_chain, 1)
                pool.wait_ge(pool_chain, n_chain[0])

            pool.dma_start(wt_rows[:, :], a["L0_cond_wt"]).then_inc(ld["small"], 16)
            pool.dma_start(small_rows[0:SEQ, :], a["cond_64"]).then_inc(ld["small"], 16)
            pool.dma_start(small_rows[SEQ:SEQ + C_EXP, :], a["L0_cond_wg"]).then_inc(ld["small"], 16)
            link(pool.memset(ident[:, :], 0.0))
            pool.affine_select(out=ident[:, :], in_=ident[:, :], compare_op=ALU.not_equal, fill=1.0, base=0,
                               pattern=[[-1, P]], channel_multiplier=1).then_inc(ready, 1)
            pool.memset(g_tok_T, 0.0).then_inc(ready, 1)
            pool.memset(wg_T[:, :], 0.0).then_inc(ready, 1)
            for t, n in ((ahead8, 8), (ahead4, 4)):
                link(pool.memset(t[:, :, :], 0.0))
                pool.affine_select(out=t[:, :, :], in_=t[:, :, :], compare_op=ALU.is_gt, fill=TINY, base=0,
                                   pattern=[[1, n], [-1, n]], channel_multiplier=0).then_inc(ready, 1)
            for t, name, rows in ((0, "L1_ffn_ln_g", 8), (8, "L1_ffn_ln_b", 8), (48, "L1_ffn_b2", 8)):
                pool.dma_start(vec_rows[t:t + rows, :], a[name]).then_inc(ld["vec"], 16)
            pool.dma_start(vec_rows[V_B1:V_B2, :], a["L1_ffn_b1"].rearrange("e (b p) -> (e b) p", p=P))\
                .then_inc(ld["vec"], 16)
            pool.dma_start(vec_rows[V_GN:V_ROWS, :], a["L1_cond_g_norm"].unsqueeze(0)).then_inc(ld["vec"], 16)
            pool.iota(pos_i[:, :], pattern=[[0, 1]], base=LEN - 1, channel_multiplier=-1).then_inc(ready, 1)
            pool.iota(iota_i[:, :], pattern=[[1, F_EXP]], base=0, channel_multiplier=0).then_inc(ready, 1)
            for n, name in enumerate(("w0", "b0", "g0", "b1", "g1")):
                src = a["L1_cond_" + name]
                src = src[0, :] if name == "w0" else src
                pool.dma_start(rp_rows[:, n, :], src.partition_broadcast(POSN)).then_inc(ld["rp"], 16)
            pool.dma_start(rp_w1[:, :], a["L1_cond_w1"]).then_inc(ld["rp"], 16)
            pool.dma_start(rp_w2[:, :], a["L1_cond_w2"]).then_inc(ld["rp"], 16)
            pool.dma_start(rp_b2[:, :], a["L1_cond_b2"].unsqueeze(1)).then_inc(ld["rp"], 16)
            pool.dma_start(gk[:, :], a["L0_ffn_gate_kernel"]).then_inc(ld["gk"], 16)
            pool.dma_start(f_bias[:, :], a["L0_ffn_gate_bias"].partition_broadcast(P)).then_inc(ld["gk"], 16)
            pool.dma_start(router_w[:, :], a["L1_ffn_router_W"]).then_inc(ld["gk"], 16)
            pool.dma_start(router_b[:, :], a["L1_ffn_router_b"].partition_broadcast(P)).then_inc(ld["gk"], 16)
            for n, name in enumerate(("q_scale", "k_scale")):
                pool.dma_start(qk_scale[:, n, :], a["L1_cond_" + name].partition_broadcast(P))\
                    .then_inc(ld["att"], 16)
            pool.dma_start(null_b[:, :], a["L1_cond_null_attn_bias"].partition_broadcast(P)).then_inc(ld["att"], 16)
            pool.dma_start(g_out[:, :], a["L1_cond_g_out"].partition_broadcast(P)).then_inc(ld["att"], 16)
            for s in range(BPT):
                pool.dma_start(mask_u8[s * LEN:(s + 1) * LEN, :, :],
                               a["mask_BxS_bf1"].rearrange("(t s) j -> s t j", s=BPT)[s].partition_broadcast(LEN))\
                    .then_inc(ld["att"], 16)
            for h in range(2):
                pool.dma_start(nv_col[h * DH:(h + 1) * DH, :], a["cond_64"][1, :].unsqueeze(1))\
                    .then_inc(ld["att"], 16)

            def split(n):
                pool.wait_ge(act_chunk, n + 1)
                c = chunks[n]
                pool.tensor_tensor(c(w_lo), c(w_stage), c(w_hi).bitcast(f32), ALU.subtract).then_inc(pool_lo, 1)

            for n in range(CH_N):
                split(n)
                if n == C_BLK:
                    pool.memset(k_diag[:, :, :, :], 0.0).then_inc(ready, 1)
                    pool.memset(v_diag[:, :, :, :], 0.0).then_inc(ready, 1)
                    pool.memset(nv_sel[:, :, :], 0.0).then_inc(ready, 1)
                    pool.memset(nv_out[:, :], 0.0).then_inc(ready, 1)
                    pool.memset(pn_T[:, :], 0.0).then_inc(ready, 1)

            pool.wait_ge(ld["gate_c"], 32)
            for s in range(HALVES):
                cols = slice(s * HW, (s + 1) * HW)
                for q in (2, 3):
                    pool.wait_ge(v_hid, C_BLK * s + q + 1)
                    pool.tensor_tensor(c_hid[:, q, cols], c_hid[:, q, cols], c_gate[:, q, cols], ALU.mult)\
                        .then_inc(pool_mul, 1)

            for s in range(HALVES):
                cols = slice(s * HW, (s + 1) * HW)
                pool.wait_ge(ld[f"gate_f{s}"], 32)
                for q in (5, 6, 7):
                    pool.wait_ge(v_hid, 2 * C_BLK + F_BLK * s + q + 1)
                    pool.tensor_tensor(f_hid[:, q, cols], f_hid[:, q, cols], f_gate[:, q, cols], ALU.mult)\
                        .then_inc(pool_mul, 1)

            pool.wait_ge(ld["bias_r"], 16 * BPT)
            for s in range(BPT):
                b = base_bias[s * LEN:(s + 1) * LEN, :, :]
                pool.affine_select(out=b, in_=b, compare_op=ALU.is_ge, fill=MASKED, base=0,
                                   pattern=[[0, HEADS], [-1, LEN]], channel_multiplier=1).then_inc(pool_bias, 1)
                pool.wait_ge(pool_bias, s + 1)

            def subtract(t):
                pool.wait_ge(v_max, t + 1)
                pool.tensor_tensor(s_buf[:, t % 2], s_buf[:, t % 2],
                                   smax[:, t % 2, :].unsqueeze(2).broadcast_to([P, HEADS, KEYS]), ALU.subtract)\
                    .then_inc(pool_sub, 1)

            def probs(t):
                pool.wait_ge(v_rs, t + 1)
                if t >= 2:
                    pool.wait_ge(v_pT, t - 1)
                pool.tensor_tensor(p_buf[:, t % 2], e_buf[:, t % 2, :, 0:LEN],
                                   ssum[:, t % 2, :].unsqueeze(2).broadcast_to([P, HEADS, LEN]), ALU.mult)\
                    .then_inc(pool_prob, 1)

            def split_w1(e):
                pool.wait_ge(act_w1, e + 1)
                c = slice(e * M_FF, (e + 1) * M_FF)
                pool.tensor_tensor(w_lo[:, c], w_stage[:, c], w_hi[:, c].bitcast(f32), ALU.subtract)\
                    .then_inc(pool_w1, 1)

            for t in range(TILES):
                subtract(t)
                if t >= 1:
                    probs(t - 1)
                split_w1(t)
            probs(TILES - 1)

            def low_input(k):
                pool.wait_ge(act_xe, 2 * (k + 1))
                if k >= 2:
                    pool.wait_ge(pe_m_up, M_BLK * (k - 1))
                pool.tensor_tensor(act_lo[:, (k % 2) * HW:(k % 2 + 1) * HW], x_exp[:, k % 2],
                                   act_hi[:, (k % 2) * HW:(k % 2 + 1) * HW].bitcast(f32), ALU.subtract)\
                    .then_inc(pool_xe, 1)

            steps = M_EXP * HALVES
            for k in range(steps + 2):
                if k < steps:
                    low_input(k)
                if k >= 2:
                    j = k - 2
                    pool.wait_ge(v_y, j + 1)
                    if j >= 2:
                        pool.wait_ge(pool_acc, j)
                        pool.tensor_tensor(y_acc[:, j % 2], y_acc[:, j % 2], y_tmp[:, j % 2], ALU.add)\
                            .then_inc(pool_acc, 1)
                    else:
                        pool.tensor_copy(y_acc[:, j % 2], y_tmp[:, j % 2]).then_inc(pool_acc, 1)

        @block.scalar
        def _(act):
            def copy_hi(n):
                act.wait_ge(v_T, n + 1)
                cols = slice(n % 2 * HW, (n % 2 + 1) * HW)
                act.activation(act_hi[:, cols], act_T[:, cols], ACT.Copy).then_inc(act_hi_s, 1)

            def chunk(n):
                act.wait_ge(ld["wc" if n < CH_F else "wf" if n < CH_Q else "wq"], 64 if n < CH_Q else 16)
                act.activation(chunks[n](w_hi), chunks[n](w_stage), ACT.Copy).then_inc(act_chunk, 1)

            act.wait_ge(v_rp, 1)
            act.activation(rp_sd[:, 0:1], rp_mv[:, 0, 1:2], ACT.Sqrt, bias=eps[0:POSN, :]).then_inc(act_rp, 1)
            chunk(0)
            for s in range(HALVES):
                copy_hi(s)
            for n in range(1, CH_F):
                chunk(n)
            act.wait_ge(v_z, 1)
            act.activation(r_s[:, :, 0:C_EXP], r_z[:, :, 0:C_EXP], ACT.Exp).then_inc(act_exp, 1)

            def gate_copy(u):
                act.wait_ge(pe_up, u + 1)
                if u >= 2:
                    act.wait_ge(v_hid, u - 1)
                act.activation(g_sb[:, u % 2], bank(2 * (u % 2)), ACT.Copy).then_inc(act_g, 1)

            for u in range(2 * C_BLK):
                gate_copy(u)
                if CH_F + u < CH_N:
                    chunk(CH_F + u)
                if u == 4:
                    act.wait_ge(v_rp, 2)
                    act.activation(rp_h[:, 1, :], rp_h[:, 0, :], ACT.Silu).then_inc(act_rp, 1)
            chunk(CH_F + 10)
            for s in range(HALVES):
                copy_hi(2 + s)
            act.wait_ge(v_rp, 4)
            act.activation(rp_sd[:, 1:2], rp_mv[:, 1, 1:2], ACT.Sqrt, bias=eps[0:POSN, :]).then_inc(act_rp, 1)
            act.wait_ge(pe_log, 2)
            act.activation(r_s[:, :, :], bank(4)[:, 0:P].rearrange("p (t e) -> p t e", e=F_EXP), ACT.Sigmoid)\
                .then_inc(act_exp, 1)
            for u in range(2 * C_BLK, 2 * C_BLK + 2 * F_BLK):
                act.wait_ge(pe_up, u + 1)
                act.wait_ge(v_hid, u - 1)
                act.activation(g_sb[:, u % 2], bank(2 * (u % 2)), ACT.Silu).then_inc(act_g, 1)
                if u == 2 * C_BLK + 1:
                    act.wait_ge(v_rp, 5)
                    act.activation(rp_h[:, 1, :], rp_h[:, 0, :], ACT.Silu).then_inc(act_rp, 1)

            for s in range(HALVES):
                act.wait_ge(v_var, s + 1)
                act.activation(std[:, s * HT:(s + 1) * HT], mv[:, s * HT:(s + 1) * HT, 1], ACT.Sqrt,
                               bias=eps[:, :]).then_inc(act_sqrt, 1)
            for s in range(HALVES):
                copy_hi(4 + s)
            act.wait_ge(v_n2, 1)
            act.activation(k2rn[:, :], k2sum[:, :], ACT.Sqrt).then_inc(act_sqrt, 1)

            def q_squares(t):
                act.wait_ge(pe_q, t + 1)
                if t >= 2:
                    act.wait_ge(v_red, t - 1)
                act.activation(q_sq[:, t % 2, :], ps[:, 2 * (t % 2):2 * (t % 2) + 2, :].rearrange("p b c -> p (b c)"),
                               ACT.Square).then_inc(act_sq, 1)
                act.wait_ge(v_red, t + 1)
                act.activation(rn[:, t, :], n2[:, t, :], ACT.Sqrt).then_inc(act_sqrt, 1)

            def q_turned(t):
                act.wait_ge(pe_qT, t + 1)
                act.activation(q_T[:, :, t * P:(t + 1) * P],
                               ps[:, 4 + 2 * (t % 2):6 + 2 * (t % 2), :].rearrange("p b (c k) -> p (b c) k", k=P),
                               ACT.Copy).then_inc(act_qT, 1)

            for t in range(TILES):
                q_squares(t)
                if t >= 1:
                    q_turned(t - 1)
            q_turned(TILES - 1)

            def att_turned(t):
                act.wait_ge(pe_av, t + 1)
                if t >= 2:
                    act.wait_ge(pe_wo, t - 1)
                act.activation(att_T[:, t % 2].rearrange("p b (s i) -> p b s i", s=BPT),
                               ps[:, 4:6, :].rearrange("p h (s b i) -> p b (h s) i", s=2, b=HB),
                               ACT.Copy).then_inc(act_attT, 1)

            def high_w1(e):
                act.wait_ge(ld["w1"], 16)
                c = slice(e * M_FF, (e + 1) * M_FF)
                act.activation(w_hi[:, c], w_stage[:, c], ACT.Copy).then_inc(act_w1, 1)

            for t in range(TILES):
                act.wait_ge(pool_sub, t + 1)
                if t >= 2:
                    act.wait_ge(pool_prob, t - 1)
                    act.wait_ge(v_pn, t - 1)
                act.activation(e_buf[:, t % 2], s_buf[:, t % 2], ACT.Exp).then_inc(act_pexp, 1)
                high_w1(t)
                if t >= 1:
                    att_turned(t - 1)
            att_turned(TILES - 1)

            for j in range(2):
                act.wait_ge(v_var, 3 + j)
                act.activation(std[:, :], mv[:, :, 1], ACT.Sqrt, bias=eps[:, :]).then_inc(act_sqrt, 1)
            act.wait_ge(v_z, 2)
            act.activation(r_s[:, :, 0:M_EXP], r_z[:, :, 0:M_EXP], ACT.Exp).then_inc(act_exp, 1)

            def expert_input(k):
                e, s = divmod(k, HALVES)
                act.wait_ge(v_T, 8)
                if k >= 2:
                    act.wait_ge(pool_xe, k - 1)
                act.activation(x_exp[:, k % 2], act_T[:, s * HW:(s + 1) * HW], ACT.Identity,
                               scale=vec[:, V_LNG + e:V_LNG + e + 1], bias=vec[:, V_LNB + e:V_LNB + e + 1])\
                    .then_inc(act_xe, 1)
                if k >= 2:
                    act.wait_ge(pe_m_up, M_BLK * (k - 1))
                act.wait_ge(act_xe, 2 * k + 1)
                act.activation(act_hi[:, (k % 2) * HW:(k % 2 + 1) * HW], x_exp[:, k % 2], ACT.Copy)\
                    .then_inc(act_xe, 1)

            steps = M_EXP * HALVES
            expert_input(0)
            expert_input(1)
            for k in range(steps):
                e = k // HALVES
                for b in range(M_BLK):
                    act.wait_ge(pe_m_up, M_BLK * k + b + 1)
                    if k >= 2:
                        act.wait_ge(pe_m_down, k - 1)
                    c = V_B1 + e * M_BLK + b
                    act.activation(gelu[:, k % 2, b, :], bank(b), ACT.Gelu, bias=vec[:, c:c + 1])\
                        .then_inc(act_gelu, 1)
                if k + 2 < steps:
                    expert_input(k + 2)

        @block.tensor
        def _(pe):
            def three(dst, w, x, n=1, first=True, last=True):
                (wh, wl), (xh, xl) = w, x
                pe.matmul(dst, wh, xh, start=first, stop=False)
                pe.matmul(dst, wh, xl, start=False, stop=False)
                return pe.matmul(dst, wl, xh, start=False, stop=last)

            def half_pair(s):
                return act_hi[:, s * HW:(s + 1) * HW], act_lo[:, s * HW:(s + 1) * HW]

            pe.wait_ge(ready, 1)
            pe.wait_ge(ld["small"], 48)
            pe.transpose(bank(7)[:, 0:C_EXP], wt_rows[:, :], ident[0:C_EXP, 0:C_EXP])
            pe.transpose(bank(7)[0:DH, 64:64 + SEQ + C_EXP], small_rows[:, :],
                         ident[0:SEQ + C_EXP, 0:SEQ + C_EXP]).then_inc(pe_small, 1)
            for s in range(HALVES):
                pe.wait_ge(ld["x"], 32)
                for t in range(HT):
                    mm = pe.transpose(bank(4 + s)[:, t * P:(t + 1) * P], x_tok[:, s * HT + t, :], ident[:, :])
                mm.then_inc(pe_xT, 1)
            pe.wait_ge(v_small, 3)
            pe.wait_ge(ld["vec"], 80)
            pe.transpose(bank(7)[:, 128:128 + V_ROWS], vec_rows[:, :], ident[0:V_ROWS, 0:V_ROWS])\
                .then_inc(pe_small, 1)
            pe.wait_ge(ready, 3)
            for t in range(TILES):
                pe.wait_ge(v_T, t // HT + 1)
                o = bank(6)[:, t * C_EXP:(t + 1) * C_EXP]
                pe.matmul(o, act_T[:, t * P:(t + 1) * P], wt_T[:, :], start=True, stop=False)
                mm = pe.matmul(o, g_tok_T[:, t * P:(t + 1) * P], wg_T[:, :], start=False, stop=True)
            mm.then_inc(pe_log, 1)

            def up_unit(u, base, blocks, s, b, hi_need, lo_need, ch):
                pe.wait_ge(act_hi_s, hi_need)
                pe.wait_ge(v_lo, lo_need)
                pe.wait_ge(pool_lo, ch)
                if u >= 2:
                    pe.wait_ge(act_g, u - 1)
                    pe.wait_ge(v_hid, u - 1)
                for g in range(2):
                    c = slice(base + (g * blocks + b) * P, base + (g * blocks + b + 1) * P)
                    mm = three(bank(2 * (u % 2) + g), (w_hi[:, c], w_lo[:, c]), half_pair(s))
                mm.then_inc(pe_up, 1)

            def turn_gates(n, rows):
                pe.wait_ge(v_comb, n)
                pe.transpose(bank(5)[0:rows, 0:P], comb[:, 0:rows], ident[:, :]).then_inc(pe_comb, 1)

            def rel_turn(n):
                pe.wait_ge(act_rp, 2 * n)
                pe.transpose(bank(7)[:, 256:256 + POSN], rp_h[:, 1, :], ident[0:POSN, 0:POSN]).then_inc(pe_rp, 1)

            for u in range(2 * C_BLK):
                s, b = divmod(u, C_BLK)
                up_unit(u, C0, C_BLK, s, b, s + 1, s + 1, b + 1)
                if u == 5:
                    pe.wait_ge(ld["rp"], 128)
                    pe.wait_ge(v_small, 4)
                    rel_turn(1)
                if u == 7:
                    pe.wait_ge(v_rp, 3)
                    pe.matmul(bank(7)[0:POSN, 320:448], rp_T[:, 0, :], rp_w1[:, :], start=True, stop=True)\
                        .then_inc(pe_rp, 1)
                if u == 7:
                    turn_gates(1, C_EXP * TILES)
            pe.wait_ge(ld["cd"], 32)
            for s in range(HALVES):
                if s == 1:
                    pe.wait_ge(v_rp, 4)
                order = (C_PAIRS, 0, 1, 2, 3)
                for n, b in enumerate(order):
                    if b == C_PAIRS:
                        pe.wait_ge(v_hid, C_BLK * (s + 1))
                    if b == 0:
                        pe.wait_ge(v_mul, s + 1)
                    if b >= 2 and b < C_PAIRS:
                        pe.wait_ge(pool_mul, 2 * s + b - 1)
                    mm = pe.matmul(bank(6 + s), c_down[:, b, :], c_hid[:, b, s * HW:(s + 1) * HW],
                                   start=(n == 0), stop=(n == C_BLK - 1))
                mm.then_inc(pe_down, 1)
            pe.wait_ge(ld["gk"], 64)
            for t in range(TILES):
                pe.wait_ge(v_T, 2 + t // HT + 1)
                mm = pe.matmul(bank(4)[:, t * F_EXP:(t + 1) * F_EXP], act_T[:, t * P:(t + 1) * P], gk[:, :],
                               start=True, stop=True)
            mm.then_inc(pe_log, 1)
            for j in range(2 * F_BLK):
                u = 2 * C_BLK + j
                s, b = divmod(j, F_BLK)
                up_unit(u, F0, F_BLK, s, b, 2 + s + 1, 2 + s + 1, CH_F + b + 1)
                if j == 4:
                    rel_turn(2)
                if j == 9:
                    pe.wait_ge(v_rp, 6)
                    pe.matmul(bank(7)[0:HEADS, 320:320 + POSN], rp_w2[:, :], rp_T[:, 1, :], start=True, stop=True)\
                        .then_inc(pe_rp, 1)
                if j == 10:
                    turn_gates(2, P)
            pe.wait_ge(ld["fd"], 32)
            pe.wait_ge(v_rp, 8)
            for s in range(HALVES):
                pe.wait_ge(v_hid, 2 * C_BLK + F_BLK * (s + 1))
                pe.wait_ge(v_mul, 2 + s + 1)
                pe.wait_ge(pool_mul, 4 + 3 * (s + 1))
                for t in range(HT):
                    cols = slice((s * HT + t) * P, (s * HT + t + 1) * P)
                    for b in range(F_BLK):
                        mm = pe.matmul(bank(6 + s)[:, t * P:(t + 1) * P], f_hid[:, b, cols], f_down[:, b, :],
                                       start=(b == 0), stop=(b == F_BLK - 1))
                mm.then_inc(pe_down, 1)
            pe.wait_ge(v_nv, 1)
            pe.wait_ge(ld["wo"], 16)
            for b in range(HB):
                mm = pe.matmul(bank(3)[0:HEADS, 0:P], nv_sel[:, b, :], w_out[:, b, :],
                               start=(b == 0), stop=(b == HB - 1))
            mm.then_inc(pe_nv, 1)
            for s in range(HALVES):
                pe.wait_ge(v_xn, s + 1)
                for t in range(HT):
                    mm = pe.transpose(bank(4 + s)[:, t * P:(t + 1) * P], xn_tok[:, s * HT + t, :], ident[:, :])
                mm.then_inc(pe_xT, 1)
            pe.wait_ge(ld["kv"], 16)
            for s in range(HALVES):
                pe.wait_ge(v_T, 4 + s + 1)
                for t in range(HT):
                    cols = slice((s * HT + t) * P, (s * HT + t + 1) * P)
                    mm = pe.matmul(bank(6 + s)[:, t * P:(t + 1) * P], act_T[:, cols], w_kv[:, :],
                                   start=True, stop=True)
                mm.then_inc(pe_kv, 1)

            def q_rows(t):
                pe.wait_ge(act_hi_s, 4 + t // HT + 1)
                pe.wait_ge(v_lo, 4 + t // HT + 1)
                pe.wait_ge(pool_lo, CH_N)
                if t == 0:
                    pe.wait_ge(v_kd, 1)
                if t == 1:
                    pe.wait_ge(v_kd, 1)
                if t >= 2:
                    pe.wait_ge(v_qhat, t - 1)
                cols = slice(t * P, (t + 1) * P)
                for j in range(2):
                    c = slice(Q0 + j * HW, Q0 + (j + 1) * HW)
                    mm = three(bank(2 * (t % 2) + j), (act_hi[:, cols], act_lo[:, cols]), (w_hi[:, c], w_lo[:, c]))
                mm.then_inc(pe_q, 1)

            def q_turn(t):
                pe.wait_ge(v_qhat, t + 1)
                pe.wait_ge(v_kv, 1)
                if t >= 2:
                    pe.wait_ge(act_qT, t - 1)
                for b in range(HB):
                    mm = pe.transpose(bank(4 + 2 * (t % 2) + b // 4)[:, (b % 4) * P:(b % 4 + 1) * P],
                                      q_hat[:, t % 2, b * P:(b + 1) * P], ident[:, :])
                mm.then_inc(pe_qT, 1)

            pe.wait_ge(v_k, 1)
            pe.wait_ge(v_nv, 2)
            for t in range(TILES + 1):
                mm = pe.transpose(bank(t // HT)[:, (t % HT) * P:(t % HT + 1) * P],
                                  k_dup[:, t].rearrange("p u d -> p (u d)"), ident[:, :])
            mm.then_inc(pe_kT, 1)
            q_rows(0)
            for t in range(TILES):
                if t + 1 < TILES:
                    q_rows(t + 1)
                q_turn(t)

            def scores(t):
                pe.wait_ge(act_qT, TILES)
                if t >= 2:
                    pe.wait_ge(v_max, t - 1)
                if t < 2:
                    pe.wait_ge(v_qhat, TILES)
                pe.wait_ge(v_kd, 1)
                for b in range(HB):
                    for s in range(BPT):
                        mm = pe.matmul(ps[s * LEN:(s + 1) * LEN, 2 * (t % 2) + b // 4,
                                          (b % 4) * 2 * KEYS:(b % 4 + 1) * 2 * KEYS],
                                       q_T[:, b, t * P + s * LEN:t * P + (s + 1) * LEN],
                                       k_diag[:, t * BPT + s].rearrange("p u k -> p (u k)"), start=True, stop=True)
                mm.then_inc(pe_sim, 1)

            def null_turn(t):
                pe.wait_ge(v_pn, t + 1)
                pe.transpose(bank(7)[0:HEADS, 0:P], p_null[:, t % 2, :], ident[:, :]).then_inc(pe_pn, 1)

            def values(t):
                pe.wait_ge(v_pT, t + 1)
                if t >= 1:
                    pe.wait_ge(act_attT, t)
                for s in range(BPT):
                    for h in range(2):
                        mm = pe.matmul(ps[h * DH:(h + 1) * DH, 4 + s // 2,
                                          (s % 2) * HB * LEN:(s % 2 + 1) * HB * LEN],
                                       v_diag[:, t, s, :],
                                       pT_buf[:, t % 2].rearrange("p (b u) i -> p u b i", u=2)[:, h],
                                       start=True, stop=True)
                mm.then_inc(pe_av, 1)

            def project(t):
                pe.wait_ge(act_attT, t + 1)
                pe.wait_ge(v_pn, t + 1)
                pe.wait_ge(v_nv, 3 + t)
                if t >= 1:
                    pe.wait_ge(v_wo, t)
                for b in range(HB):
                    pe.matmul(bank(6)[:, 0:P], att_T[:, t % 2, b, :], w_out[:, b, :], start=(b == 0), stop=False)
                pe.matmul(bank(6)[:, 0:P], pn_T[:, :], nv_out[:, :], start=False, stop=True).then_inc(pe_wo, 1)

            scores(0)
            scores(1)
            for t in range(TILES):
                null_turn(t)
                values(t)
                if t + 2 < TILES:
                    scores(t + 2)
                project(t)

            for s in range(HALVES):
                pe.wait_ge(v_xn, 3)
                for t in range(HT):
                    mm = pe.transpose(bank(4 + s)[:, t * P:(t + 1) * P], xc[:, s * HT + t, :], ident[:, :])
                mm.then_inc(pe_xT, 1)
            for t in range(TILES):
                pe.wait_ge(v_T, 6 + t // HT + 1)
                mm = pe.matmul(bank(6)[:, 256 + t * M_EXP:256 + (t + 1) * M_EXP], act_T[:, t * P:(t + 1) * P],
                               router_w[:, :], start=True, stop=True)
            mm.then_inc(pe_log, 1)
            pe.wait_ge(v_xn, 4)
            for s in range(HALVES):
                pe.wait_ge(v_T, 7 + s)
                for t in range(HT):
                    mm = pe.transpose(bank(4 + s)[:, t * P:(t + 1) * P], xh_tok[:, s * HT + t, :], ident[:, :])
                mm.then_inc(pe_xT, 1)

            w2 = w_stage[:, 0:M_EXP * M_FF].rearrange("p (e b c) -> p e b c", e=M_EXP, c=P)

            def m_up(k):
                e = k // HALVES
                pe.wait_ge(pool_xe, k + 1)
                r = k % 2
                x = act_hi[:, r * HW:(r + 1) * HW], act_lo[:, r * HW:(r + 1) * HW]
                for b in range(M_BLK):
                    if k >= 1:
                        pe.wait_ge(act_gelu, M_BLK * (k - 1) + b + 1)
                    c = slice(e * M_FF + b * P, e * M_FF + (b + 1) * P)
                    three(bank(b), (w_hi[:, c], w_lo[:, c]), x).then_inc(pe_m_up, 1)

            def m_down(k):
                e = k // HALVES
                pe.wait_ge(ld["w2"], 16 * M_EXP)
                if k >= 2:
                    pe.wait_ge(v_y, k - 1)
                for b in range(M_BLK):
                    pe.wait_ge(act_gelu, M_BLK * k + b + 1)
                    mm = pe.matmul(bank(6 + k % 2), w2[:, e, b, :], gelu[:, k % 2, b, :],
                                   start=(b == 0), stop=(b == M_BLK - 1))
                mm.then_inc(pe_m_down, 1)

            steps = M_EXP * HALVES
            m_up(0)
            for k in range(steps):
                if k + 1 < steps:
                    m_up(k + 1)
                if k == 0:
                    pe.wait_ge(v_T, 10)
                    turn_gates(3, M_EXP * TILES)
                m_down(k)
            pe.wait_ge(v_combT, 3)
            for s in range(HALVES):
                pe.wait_ge(pool_acc, steps - 1 + s)
                for t in range(HT):
                    mm = pe.transpose(bank(4 + s)[:, t * P:(t + 1) * P], y_acc[:, s, t * P:(t + 1) * P], ident[:, :])
                mm.then_inc(pe_fin, 1)

        @block.vector
        def _(dve):
            n_chain = [0]

            def link(ins):
                n_chain[0] += 1
                ins.then_inc(v_chain, 1)
                dve.wait_ge(v_chain, n_chain[0])

            def turned(s, src, base, scale=None, lo=True):
                cols = slice(s * HW, (s + 1) * HW)
                if scale is None:
                    dve.tensor_copy(act_T[:, cols], src).then_inc(v_T, 1)
                else:
                    dve.tensor_scalar(act_T[:, cols], src, scale, None, ALU.mult).then_inc(v_T, 1)
                if lo:
                    dve.wait_ge(v_T, base + s + 1)
                    dve.wait_ge(act_hi_s, base + s + 1)
                    dve.tensor_tensor(act_lo[:, cols], act_T[:, cols], act_hi[:, cols].bitcast(f32), ALU.subtract)\
                        .then_inc(v_lo, 1)

            link(dve.memset(eps[:, :], LN_EPS))
            dve.wait_ge(ready, 7)
            dve.wait_ge(ld["rp"], 128)
            dve.tensor_copy(iota16[:, :], iota_i[:, :])
            link(dve.tensor_copy(pos[:, :], pos_i[:, :]))
            link(dve.scalar_tensor_tensor(rp_h[:, 0, :], rp_rows[:, 0, :], pos[:, 0:1], rp_rows[:, 1, :],
                                          ALU.mult, ALU.add))
            link(dve.bn_stats(rp_st[:, :], rp_h[:, 0, :]))
            dve.bn_aggr(rp_mv[:, 0, :], rp_st[:, :]).then_inc(v_rp, 1)

            dve.wait_ge(pe_small, 1)
            dve.wait_ge(ready, 5)
            dve.tensor_copy(wt_T[:, :], bank(7)[:, 0:C_EXP]).then_inc(v_small, 1)
            dve.tensor_copy(g_tok_T[0:DH, :].rearrange("p (b i) -> p b i", i=LEN),
                            bank(7)[0:DH, 64:64 + SEQ].unsqueeze(2).broadcast_to([DH, SEQ, LEN]))\
                .then_inc(v_small, 1)
            dve.tensor_copy(wg_T[0:DH, :], bank(7)[0:DH, 64 + SEQ:64 + SEQ + C_EXP]).then_inc(v_small, 1)
            for s in range(HALVES):
                dve.wait_ge(pe_xT, s + 1)
                turned(s, bank(4 + s), 0)
            dve.wait_ge(pe_small, 2)
            dve.tensor_copy(vec[:, :], bank(7)[:, 128:128 + V_ROWS]).then_inc(v_small, 1)

            def c_unit(u):
                s, b = divmod(u, C_BLK)
                dve.wait_ge(act_g, u + 1)
                if u >= 2:
                    dve.wait_ge(v_hid, u - 1)
                link(dve.scalar_tensor_tensor(g_lk[:, u % 2], g_sb[:, u % 2], 0.01, g_sb[:, u % 2], ALU.mult, ALU.max))
                dve.tensor_tensor(c_hid[:, b, s * HW:(s + 1) * HW], g_lk[:, u % 2], bank(2 * (u % 2) + 1), ALU.mult)\
                    .then_inc(v_hid, 1)

            z, e8 = r_z[:, :, 0:8], r_s[:, :, 0:8]

            def bc(x, n=8):
                return x.unsqueeze(2).broadcast_to([P, TILES, n])

            def rank8(v):
                big = r_big[:, :].rearrange("p (t e f) -> p t e f", e=8, f=8)
                link(dve.tensor_tensor(big, v.unsqueeze(2).broadcast_to([P, TILES, 8, 8]),
                                       v.unsqueeze(3).broadcast_to([P, TILES, 8, 8]), ALU.subtract))
                link(dve.tensor_tensor(big, big, ahead8[:, :, :].unsqueeze(1).broadcast_to([P, TILES, 8, 8]),
                                       ALU.is_ge))
                link(dve.tensor_reduce(r_rank[:, :, 0:8], big, AX, ALU.add))

            dve.wait_ge(pe_log, 1)
            link(dve.tensor_scalar(z, bank(6)[:, 0:64].rearrange("p (t e) -> p t e", e=8), 0.5, None, ALU.mult))
            link(dve.tensor_reduce(r_sum[:, :], z, AX, ALU.max))
            dve.tensor_tensor(z, z, bc(r_sum[:, :]), ALU.subtract).then_inc(v_z, 1)
            c_unit(0)
            dve.wait_ge(act_exp, 1)
            link(dve.tensor_reduce(r_sum[:, :], e8, AX, ALU.add))
            link(dve.reciprocal(r_inv[:, :], r_sum[:, :]))
            link(dve.tensor_tensor(e8, e8, bc(r_inv[:, :]), ALU.mult))
            c_unit(1)
            rank8(e8)
            c_unit(2)
            link(dve.scalar_tensor_tensor(z, r_rank[:, :, 0:8], 1.5, e8, ALU.is_lt, ALU.mult))
            link(dve.tensor_reduce(r_sum[:, :], z, AX, ALU.add))
            link(dve.tensor_scalar(r_sum[:, :], r_sum[:, :], 1e-20, None, ALU.add))
            link(dve.reciprocal(r_inv[:, :], r_sum[:, :]))
            dve.tensor_tensor(comb[:, 0:64].rearrange("p (e t) -> p t e", t=TILES), z, bc(r_inv[:, :]), ALU.mult)\
                .then_inc(v_comb, 1)
            c_unit(3)

            def rp_norm(n, sig):
                dve.wait_ge(act_rp, sig)
                link(dve.reciprocal(rp_sd[:, n:n + 1], rp_sd[:, n:n + 1]))
                link(dve.tensor_scalar(rp_h[:, 0, :], rp_h[:, 0, :], rp_mv[:, n, 0:1], rp_sd[:, n:n + 1],
                                       ALU.subtract, ALU.mult))
                dve.tensor_tensor(rp_h[:, 0, :], rp_h[:, 0, :], rp_rows[:, 2 + 2 * n, :], ALU.mult).then_inc(v_rp, 1)

            rp_norm(0, 1)
            c_unit(4)
            c_unit(5)
            dve.wait_ge(pe_rp, 1)
            dve.tensor_copy(rp_T[:, 0, :], bank(7)[:, 256:256 + POSN]).then_inc(v_rp, 1)
            c_unit(6)
            c_unit(7)
            dve.wait_ge(pe_rp, 2)
            link(dve.tensor_tensor(rp_h[:, 0, :], bank(7)[0:POSN, 320:448], rp_rows[:, 3, :], ALU.add))
            link(dve.bn_stats(rp_st[:, :], rp_h[:, 0, :]))
            dve.bn_aggr(rp_mv[:, 1, :], rp_st[:, :]).then_inc(v_rp, 1)
            dve.wait_ge(pe_comb, 1)
            dve.tensor_copy(comb_T[0:64, :], bank(5)[0:64, 0:P]).then_inc(v_combT, 1)
            c_unit(8)
            c_unit(9)
            dve.wait_ge(ld["gate_c"], 32)
            for s in range(HALVES):
                cols = slice(s * HW, (s + 1) * HW)
                for q in (0, 1):
                    dve.wait_ge(v_hid, C_BLK * s + q + 1)
                    ins = dve.tensor_tensor(c_hid[:, q, cols], c_hid[:, q, cols], c_gate[:, q, cols], ALU.mult)
                ins.then_inc(v_mul, 1)
            for s in range(HALVES):
                dve.wait_ge(pe_down, s + 1)
                turned(s, bank(6 + s), 2)

            rp_norm(1, 3)

            def f_unit(u):
                s, b = divmod(u, F_BLK)
                n = 2 * C_BLK + u
                dve.wait_ge(act_g, n + 1)
                dve.tensor_tensor(f_hid[:, b, s * HW:(s + 1) * HW], g_sb[:, n % 2], bank(2 * (n % 2) + 1), ALU.mult)\
                    .then_inc(v_hid, 1)

            f_unit(0)
            f_unit(1)
            dve.wait_ge(act_exp, 2)
            dve.wait_ge(ld["gk"], 64)
            link(dve.tensor_tensor(r_s[:, :, :], r_s[:, :, :], f_bias[:, :].unsqueeze(1).broadcast_to([P, TILES, 16]),
                                   ALU.add))
            g4 = r_s[:, :, :].rearrange("p t (g k) -> p t g k", k=4)
            ma, mb, lo_a, lo_b = r_a[:, :, :], r_b[:, :, :], r_c[:, :, :], r_d[:, :, :]
            dve.tensor_tensor(ma, g4[:, :, :, 0], g4[:, :, :, 1], ALU.max)
            dve.tensor_tensor(mb, g4[:, :, :, 2], g4[:, :, :, 3], ALU.max)
            dve.tensor_tensor(lo_a, g4[:, :, :, 0], g4[:, :, :, 1], ALU.min)
            link(dve.tensor_tensor(lo_b, g4[:, :, :, 2], g4[:, :, :, 3], ALU.min))
            link(dve.tensor_tensor(lo_a, lo_a, lo_b, ALU.max))
            link(dve.tensor_tensor(lo_b, ma, mb, ALU.min))
            link(dve.tensor_tensor(lo_a, lo_a, lo_b, ALU.max))
            link(dve.tensor_tensor(ma, ma, mb, ALU.max))
            link(dve.tensor_tensor(ma, ma, lo_a, ALU.add))
            f_unit(2)
            big4 = r_big[:, 0:P].rearrange("p (t e f) -> p t e f", e=4, f=4)
            link(dve.tensor_tensor(big4, ma.unsqueeze(2).broadcast_to([P, TILES, 4, 4]),
                                   ma.unsqueeze(3).broadcast_to([P, TILES, 4, 4]), ALU.subtract))
            link(dve.tensor_tensor(big4, big4, ahead4[:, :, :].unsqueeze(1).broadcast_to([P, TILES, 4, 4]), ALU.is_ge))
            link(dve.tensor_reduce(mb, big4, AX, ALU.add))
            link(dve.tensor_scalar(mb, mb, 1.5, None, ALU.is_lt))
            f_unit(3)
            link(dve.tensor_tensor(r_z[:, :, :].rearrange("p t (g k) -> p t g k", k=4), g4,
                                   mb.unsqueeze(3).broadcast_to([P, TILES, 4, 4]), ALU.mult))
            for t in range(TILES):
                dve.max(r_max[:, t, :], r_z[:, t, :])
            f_unit(4)
            dve.wait_ge(v_hid, 2 * C_BLK + 5)
            for t in range(TILES):
                ins = dve.max_index(r_idx[:, t, :], r_max[:, t, :], r_z[:, t, :])
            link(ins)
            f_unit(5)
            link(dve.tensor_copy(r_idf[:, :, :], r_idx[:, :, :]))
            bigk = r_big[:, :].rearrange("p (t e k) -> p t e k", e=16, k=4)
            link(dve.tensor_tensor(bigk, r_idf[:, :, 0:4].unsqueeze(2).broadcast_to([P, TILES, 16, 4]),
                                   iota16[:, :].unsqueeze(1).unsqueeze(3).broadcast_to([P, TILES, 16, 4]),
                                   ALU.is_equal))
            link(dve.tensor_reduce(r_m[:, :, :], bigk, AX, ALU.add))
            f_unit(6)
            link(dve.tensor_tensor(r_z[:, :, :], r_z[:, :, :], r_m[:, :, :], ALU.mult))
            link(dve.tensor_reduce(r_sum[:, :], r_z[:, :, :], AX, ALU.add))
            link(dve.tensor_scalar(r_sum[:, :], r_sum[:, :], 1e-20, None, ALU.add))
            link(dve.reciprocal(r_inv[:, :], r_sum[:, :]))
            link(dve.tensor_tensor(r_z[:, :, :], r_z[:, :, :], bc(r_inv[:, :], 16), ALU.mult))
            dve.tensor_scalar(comb[:, :].rearrange("p (e t) -> p t e", t=TILES), r_z[:, :, :], F_SCALE, None, ALU.mult)\
                .then_inc(v_comb, 1)
            f_unit(7)
            dve.wait_ge(pe_rp, 3)
            dve.tensor_copy(rp_T[:, 1, :], bank(7)[:, 256:256 + POSN]).then_inc(v_rp, 1)
            for u in range(8, 16):
                f_unit(u)
                if u == 10:
                    dve.wait_ge(pe_rp, 4)
                    dve.tensor_scalar(rp_out[:, :], bank(7)[0:HEADS, 320:320 + POSN], rp_b2[:, 0:1], None, ALU.add)\
                        .then_inc(v_rp, 2)
                if u == 11:
                    dve.wait_ge(pe_comb, 2)
                    dve.tensor_copy(comb_T[:, :], bank(5)[:, 0:P]).then_inc(v_combT, 1)
            f_unit(16)
            f_unit(17)
            for s in range(HALVES):
                cols = slice(s * HW, (s + 1) * HW)
                dve.wait_ge(ld[f"gate_f{s}"], 32)
                for q in range(5):
                    dve.wait_ge(v_hid, 2 * C_BLK + F_BLK * s + q + 1)
                    ins = dve.tensor_tensor(f_hid[:, q, cols], f_hid[:, q, cols], f_gate[:, q, cols], ALU.mult)
                ins.then_inc(v_mul, 1)
            dve.wait_ge(ld["att"], 160)
            link(dve.tensor_scalar(mask_add[:, :, :], mask_u8[:, :, :], 1.0, -MASKED, ALU.subtract, ALU.mult))
            dve.tensor_copy(att_bias[:, :, :, LEN], null_b[:, :].unsqueeze(1).broadcast_to([P, TILES, HEADS]))
            dve.wait_ge(pool_bias, BPT)
            for t in range(TILES):
                ins = dve.tensor_tensor(att_bias[:, t, :, 0:LEN], base_bias[:, :, :],
                                        mask_add[:, t, :].unsqueeze(1).broadcast_to([P, HEADS, LEN]), ALU.add)
            ins.then_inc(v_bias, 1)
            link(dve.tensor_tensor(s_dup[:, :], qk_scale[:, 0, :], qk_scale[:, 1, :], ALU.mult))
            link(dve.tensor_scalar(s_dup[:, :], s_dup[:, :], ATT_SCALE, None, ALU.mult))
            dve.wait_ge(ready, 12)
            for h in range(2):
                rows = slice(h * DH, (h + 1) * DH)
                dst = nv_sel[rows, :, :].rearrange("p b h -> p (b h)")[:, h:h + 18 * 7 + 1:18]
                ins = dve.tensor_copy(dst, nv_col[rows, 0:1].broadcast_to([DH, HB]))
            ins.then_inc(v_nv, 1)
            for s in range(HALVES):
                dve.wait_ge(pe_down, 2 + s + 1)
                tiles = range(s * HT, (s + 1) * HT)
                xs = x_tok[:, s * HT:(s + 1) * HT, :].rearrange("p t c -> p (t c)")
                link(dve.tensor_tensor(xs, xs, bank(6 + s), ALU.add))
                for t in tiles:
                    ins = dve.bn_stats(st6[:, s, t % HT, :], x_tok[:, t, :])
                link(ins)
                for t in tiles:
                    ins = dve.bn_aggr(mv[:, t, :], st6[:, s, t % HT, :])
                ins.then_inc(v_var, 1)
            for s in range(HALVES):
                dve.wait_ge(act_sqrt, s + 1)
                link(dve.reciprocal(rstd[:, s * HT:(s + 1) * HT], std[:, s * HT:(s + 1) * HT]))
                for t in range(s * HT, (s + 1) * HT):
                    ins = dve.tensor_scalar(xn_tok[:, t, :], x_tok[:, t, :], mv[:, t, 0:1], rstd[:, t:t + 1],
                                            ALU.subtract, ALU.mult)
                ins.then_inc(v_xn, 1)
            dve.wait_ge(pe_nv, 1)
            dve.tensor_copy(nv_out[0:HEADS, :], bank(3)[0:HEADS, 0:P]).then_inc(v_nv, 1)
            for s in range(HALVES):
                dve.wait_ge(pe_xT, 2 + s + 1)
                turned(s, bank(4 + s), 4, scale=vec[:, V_GN:V_GN + 1])
            for s in range(HALVES):
                dve.wait_ge(pe_kv, s + 1)
                kv = bank(6 + s).rearrange("p (t c) -> p t c", c=P)
                dve.tensor_copy(k_tok[:, s * HT:(s + 1) * HT, :], kv[:, :, 0:DH])
                for q in range(BPT):
                    rows = slice(q * LEN, (q + 1) * LEN)
                    ins = dve.tensor_copy(v_diag[rows, s * HT:(s + 1) * HT, q, :], kv[rows, :, DH:P])
            ins.then_inc(v_kv, 1)
            dve.wait_ge(v_kv, 1)
            dve.wait_ge(ld["null"], 16)
            link(dve.tensor_tensor(k_sq, k_tok, k_tok, ALU.mult))
            dve.tensor_reduce(k2sum[:, :], k_sq, AX, ALU.add).then_inc(v_n2, 1)
            dve.wait_ge(act_sqrt, 3)
            link(dve.tensor_scalar(k2rn[:, :], k2rn[:, :], NORM_EPS, None, ALU.max))
            link(dve.reciprocal(k2rn[:, :], k2rn[:, :]))
            link(dve.tensor_tensor(k_tok, k_tok, k2rn[:, :].unsqueeze(2).broadcast_to([P, TILES + 1, DH]), ALU.mult))
            for h in range(2):
                ins = dve.tensor_tensor(k_dup[:, :, h, :], k_tok,
                                        s_dup[:, :].unsqueeze(1).broadcast_to([P, TILES + 1, DH]), ALU.mult)
            ins.then_inc(v_k, 1)
            dve.wait_ge(pe_kT, 1)
            for h in range(2):
                rows = slice(h * DH, (h + 1) * DH)
                for s in range(HALVES):
                    dve.tensor_copy(k_diag[rows, s * HT * BPT:(s + 1) * HT * BPT, h, 0:LEN],
                                    bank(s)[rows, :].rearrange("p (b k) -> p b k", k=LEN))
                ins = dve.tensor_copy(k_diag[rows, :, h, LEN], bank(2)[rows, 0:SEQ])
            ins.then_inc(v_kd, 1)

            def q_norm(t):
                dve.wait_ge(act_sq, t + 1)
                dve.tensor_reduce(n2[:, t, :], q_sq[:, t % 2, :].rearrange("p (h d) -> p h d", d=DH), AX, ALU.add)\
                    .then_inc(v_red, 1)
                dve.wait_ge(act_sqrt, 4 + t)
                link(dve.tensor_scalar(rn[:, t, :], rn[:, t, :], NORM_EPS, None, ALU.max))
                link(dve.reciprocal(rn[:, t, :], rn[:, t, :]))
                if t >= 2:
                    dve.wait_ge(pe_qT, t - 1)
                dve.tensor_tensor(q_hat[:, t % 2, :].rearrange("p (h d) -> p h d", d=DH),
                                  ps[:, 2 * (t % 2):2 * (t % 2) + 2, :].rearrange("p b (h d) -> p (b h) d", d=DH),
                                  rn[:, t, :].unsqueeze(2).broadcast_to([P, HEADS, DH]), ALU.mult)\
                    .then_inc(v_qhat, 1)

            for t in range(TILES):
                q_norm(t)

            def scored(t):
                dve.wait_ge(pe_sim, t + 1)
                if t >= 2:
                    dve.wait_ge(act_pexp, t - 1)
                if t == 0:
                    dve.wait_ge(pe_qT, TILES)
                link(dve.tensor_tensor(s_buf[:, t % 2].rearrange("p (g h) k -> p g (h k)", g=2),
                                       ps[:, 2 * (t % 2):2 * (t % 2) + 2, 0:8 * KEYS],
                                       att_bias[:, t].rearrange("p (g h) k -> p g (h k)", g=2), ALU.add))
                dve.tensor_reduce(smax[:, t % 2, :], s_buf[:, t % 2], AX, ALU.max).then_inc(v_max, 1)

            def summed(t):
                dve.wait_ge(act_pexp, t + 1)
                if t >= 2:
                    dve.wait_ge(pool_prob, t - 1)
                link(dve.tensor_reduce(ssum[:, t % 2, :], e_buf[:, t % 2], AX, ALU.add))
                dve.reciprocal(ssum[:, t % 2, :], ssum[:, t % 2, :]).then_inc(v_rs, 1)
                dve.wait_ge(v_rs, t + 1)
                if t >= 2:
                    dve.wait_ge(pe_pn, t - 1)
                dve.tensor_tensor(p_null[:, t % 2, :], e_buf[:, t % 2, :, LEN], ssum[:, t % 2, :], ALU.mult)\
                    .then_inc(v_pn, 1)

            def turned_probs(t):
                dve.wait_ge(pool_prob, t + 1)
                if t >= 2:
                    dve.wait_ge(pe_av, t - 1)
                dve.transpose(pT_buf[:, t % 2].rearrange("p h k -> p (h k)"),
                              p_buf[:, t % 2].rearrange("p h k -> p (h k)")).then_inc(v_pT, 1)
                dve.wait_ge(pe_pn, t + 1)
                if t >= 1:
                    dve.wait_ge(pe_wo, t)
                dve.tensor_copy(pn_T[0:HEADS, :], bank(7)[0:HEADS, 0:P]).then_inc(v_nv, 1)

            def projected(t):
                dve.wait_ge(pe_wo, t + 1)
                dve.tensor_copy(xc[:, t, :], bank(6)[:, 0:P]).then_inc(v_wo, 1)
                dve.wait_ge(v_wo, t + 1)
                link(dve.bn_stats(st6[:, 0, 0, :], xc[:, t, :]))
                ins = dve.bn_aggr(mv[:, t, :], st6[:, 0, 0, :])
                if t == TILES - 1:
                    ins.then_inc(v_var, 1)

            scored(0)
            for t in range(TILES):
                if t + 1 < TILES:
                    scored(t + 1)
                summed(t)
                if t >= 1:
                    projected(t - 1)
                turned_probs(t)
            projected(TILES - 1)
            dve.wait_ge(act_sqrt, 3 + TILES + 1)
            link(dve.reciprocal(rstd[:, :], std[:, :]))
            for t in range(TILES):
                ins = dve.tensor_scalar(xc[:, t, :], xc[:, t, :], mv[:, t, 0:1], rstd[:, t:t + 1],
                                        ALU.subtract, ALU.mult)
            link(ins)
            dve.tensor_tensor(xc[:, :, :], xc[:, :, :], g_out[:, :].unsqueeze(1).broadcast_to([P, TILES, P]), ALU.mult)\
                .then_inc(v_xn, 1)
            dve.wait_ge(v_xn, 3)
            for t in range(TILES):
                ins = dve.bn_stats(st6[:, t // HT, t % HT, :], xc[:, t, :])
            link(ins)
            for t in range(TILES):
                ins = dve.bn_aggr(mv[:, t, :], st6[:, t // HT, t % HT, :])
            ins.then_inc(v_var, 1)
            for s in range(HALVES):
                dve.wait_ge(pe_xT, 4 + s + 1)
                turned(s, bank(4 + s), 6, lo=False)
            dve.wait_ge(act_sqrt, 3 + TILES + 2)
            link(dve.reciprocal(rstd[:, :], std[:, :]))
            for t in range(TILES):
                ins = dve.tensor_scalar(xh_tok[:, t, :], xc[:, t, :], mv[:, t, 0:1], rstd[:, t:t + 1],
                                        ALU.subtract, ALU.mult)
            ins.then_inc(v_xn, 1)
            dve.wait_ge(pe_log, 3)
            link(dve.tensor_tensor(z, bank(6)[:, 256:320].rearrange("p (t e) -> p t e", e=8),
                                   router_b[:, :].unsqueeze(1).broadcast_to([P, TILES, 8]), ALU.add))
            for s in range(HALVES):
                dve.wait_ge(pe_xT, 6 + s + 1)
                turned(s, bank(4 + s), 8, lo=False)
            rank8(z)
            link(dve.tensor_reduce(r_sum[:, :], z, AX, ALU.max))
            dve.tensor_tensor(z, z, bc(r_sum[:, :]), ALU.subtract).then_inc(v_z, 1)
            dve.wait_ge(act_exp, 3)
            link(dve.scalar_tensor_tensor(z, r_rank[:, :, 0:8], 1.5, e8, ALU.is_lt, ALU.mult))
            link(dve.tensor_reduce(r_sum[:, :], z, AX, ALU.add))
            link(dve.reciprocal(r_inv[:, :], r_sum[:, :]))
            link(dve.tensor_tensor(z, z, bc(r_inv[:, :]), ALU.mult))
            dve.tensor_copy(comb[:, 0:64].rearrange("p (e t) -> p t e", t=TILES), z).then_inc(v_comb, 1)
            link(dve.tensor_reduce(g_sum[:, :], z, AX, ALU.add))
            dve.wait_ge(pe_comb, 3)
            dve.tensor_copy(comb_T[0:64, :], bank(5)[0:64, 0:P]).then_inc(v_combT, 1)
            for t in range(TILES):
                ins = dve.scalar_tensor_tensor(x_tok[:, t, :], xc[:, t, :], g_sum[:, t:t + 1], x_tok[:, t, :],
                                               ALU.mult, ALU.add)
            link(ins)
            steps = M_EXP * HALVES
            for k in range(steps):
                e, s = divmod(k, HALVES)
                dve.wait_ge(pe_m_down, k + 1)
                dve.wait_ge(m_gate_in[e], 16)
                if k >= 2:
                    dve.wait_ge(pool_acc, k - 1)
                dve.scalar_tensor_tensor(y_tmp[:, k % 2], bank(6 + k % 2), vec[:, V_B2 + e:V_B2 + e + 1],
                                         m_gate[:, e, s * HW:(s + 1) * HW], ALU.add, ALU.mult).then_inc(v_y, 1)
            for s in range(HALVES):
                dve.wait_ge(pe_fin, s + 1)
                xs = x_tok[:, s * HT:(s + 1) * HT, :].rearrange("p t c -> p (t c)")
                dve.tensor_tensor(xs, xs, bank(4 + s), ALU.add).then_inc(v_out, 1)


_INS = ['x', 'cond_64', 'mask_BxS_bf1', 'L0_cond_wt', 'L0_cond_wg', 'L0_cond_w_gate', 'L0_cond_w_up',
        'L0_cond_w_down', 'L0_cond_sw_gate', 'L0_cond_sw_up', 'L0_cond_sw_down', 'L0_ffn_gate_kernel',
        'L0_ffn_gate_bias', 'L0_ffn_w_gate', 'L0_ffn_w_up', 'L0_ffn_w_down', 'L0_ffn_sw_gate', 'L0_ffn_sw_up',
        'L0_ffn_sw_down', 'L1_cond_g_norm', 'L1_cond_Wq', 'L1_cond_Wkv', 'L1_cond_q_scale', 'L1_cond_k_scale',
        'L1_cond_null_attn_bias', 'L1_cond_w0', 'L1_cond_b0', 'L1_cond_g0', 'L1_cond_w1', 'L1_cond_b1',
        'L1_cond_g1', 'L1_cond_w2', 'L1_cond_b2', 'L1_cond_Wout', 'L1_cond_g_out', 'L1_ffn_router_W',
        'L1_ffn_router_b', 'L1_ffn_ln_g', 'L1_ffn_ln_b', 'L1_ffn_W1', 'L1_ffn_b1', 'L1_ffn_W2', 'L1_ffn_b2']


def kernel(**inputs):
    import numpy as _np
    import concourse.bacc as _bacc
    from concourse import mybir as _mybir
    from concourse.bass_utils import run_bass_kernel_spmd as _run

    nc = _bacc.Bacc("TRN2", target_bir_lowering=False, num_devices=1)
    arrays, views = {}, {}
    for name in _INS:
        v = _np.ascontiguousarray(inputs[name])
        if v.dtype == _np.bool_:
            v = v.view(_np.uint8)
        arrays[f"in_{name}"] = v
        views[name] = nc.dram_tensor(f"in_{name}", v.shape, _mybir.dt.from_np(v.dtype), kind="ExternalInput").ap()
    out = nc.dram_tensor("out_0", (SEQ, LEN, P), f32, kind="ExternalOutput").ap()
    two_layers(nc, views, out)
    r = _run(nc, [arrays], core_ids=[0])
    return r.results[0]["out_0"]
```

```python
import concourse.bass as bass
from concourse import mybir
from contextlib import ExitStack

f32 = mybir.dt.float32
f32r = mybir.dt.float32r
i32 = mybir.dt.int32
u32 = mybir.dt.uint32
u8 = mybir.dt.uint8
ALU = mybir.AluOpType
ACT = mybir.ActivationFunctionType
AX = mybir.AxisListType.X

P = 128
SEQ, LEN = 32, 32
TOK = SEQ * LEN
TILES = TOK // P
HALVES = 2
HT = TILES // HALVES
HW = HT * P
BPT = P // LEN

C_EXP, C_PAIRS = 8, 4
C_BLK = C_PAIRS + 1
F_EXP, F_PAIRS = 16, 8
F_BLK = F_PAIRS + 1
F_GROUPS, F_TOPK, F_SCALE = 4, 4, 2.5
HEADS, DH = 16, 64
HB = HEADS // 2
KEYS = LEN + 1
M_EXP, M_FF = 8, 512
M_BLK = M_FF // P
POSN = 2 * LEN - 1
ATT_SCALE = 8.0
MASKED = -1e30
LN_EPS = 1e-5
NORM_EPS = 1e-12
TINY = 2e-38
PAD = 96

C0, F0, Q0 = 0, 2 * C_BLK * P, 2 * C_BLK * P + 2 * F_BLK * P
WCOLS = Q0 + HEADS * DH
V_LNG, V_LNB, V_B1, V_B2, V_GN = 0, 8, 16, 48, 56
V_ROWS = 57


def two_layers(nc, a, out):
    comb_c_dram = nc.dram_tensor("comb_c", [C_EXP, TOK], f32, kind="Internal").ap()
    comb_f_dram = nc.dram_tensor("comb_f", [F_EXP, TOK], f32, kind="Internal").ap()
    gate_m_dram = nc.dram_tensor("gate_m", [M_EXP, TOK], f32, kind="Internal").ap()
    bias_dram = nc.dram_tensor("rel_bias", [HEADS, LEN, LEN], f32, kind="Internal").ap()

    ctx = ExitStack()
    with ctx:
        def sb(name, shape, dt=f32):
            return ctx.enter_context(nc.sbuf_tensor(name, shape, dt))

        def sem(name):
            return ctx.enter_context(nc.semaphore(name))

        x_tok = sb("x_tok", [P, TILES, P])
        xc = sb("xc", [P, TILES, P])
        act_T = sb("act_T", [P, TOK])
        act_hi = sb("act_hi", [P, TOK], f32r)
        act_lo = sb("act_lo", [P, TOK], f32r)
        w_stage = sb("w_stage", [P, WCOLS])
        w_hi = sb("w_hi", [P, WCOLS], f32r)
        w_lo = sb("w_lo", [P, WCOLS], f32r)
        c_down = sb("c_down", [P, C_BLK, P])
        f_down = sb("f_down", [P, F_BLK, P])
        w_out = sb("w_out", [P, HB, P])
        w_kv = sb("w_kv", [P, 2 * DH])
        arena2 = sb("arena2", [P, 8192])
        att_bias = sb("att_bias", [P, TILES, HEADS, KEYS])
        base_bias = sb("base_bias", [P, HEADS, LEN])
        v_diag = sb("v_diag", [P, TILES, BPT, DH])
        k_diag = sb("k_diag", [P, SEQ, 2, KEYS])
        ident = sb("ident", [P, P])
        vec_rows = sb("vec_rows", [V_ROWS, P])
        vec = sb("vec", [P, V_ROWS])
        small_rows = sb("small_rows", [SEQ + C_EXP, DH])
        wt_rows = sb("wt_rows", [C_EXP, P])
        wt_T = sb("wt_T", [P, PAD])
        wg_T = sb("wg_T", [P, PAD])
        gk = sb("gk", [P, PAD])
        router_w = sb("router_w", [P, PAD])
        router_b = sb("router_b", [P, M_EXP])
        f_bias = sb("f_bias", [P, F_EXP])
        rp_w1 = sb("rp_w1", [P, P])
        rp_w2 = sb("rp_w2", [P, HEADS])
        rp_b2 = sb("rp_b2", [HEADS, 1])
        rp_T = sb("rp_T", [P, 2, POSN])
        rp_out = sb("rp_out", [HEADS, POSN])
        pos_i = sb("pos_i", [POSN, 1], i32)
        pos = sb("pos", [POSN, 1])
        g_out = sb("g_out", [P, P])
        qk_scale = sb("qk_scale", [P, 2, DH])
        s_dup = sb("s_dup", [P, DH])
        null_b = sb("null_b", [P, HEADS])
        nv_col = sb("nv_col", [P, 1])
        nv_sel = sb("nv_sel", [P, HB, HEADS])
        nv_out = sb("nv_out", [P, P])
        pn_T = sb("pn_T", [P, P])
        mask_u8 = sb("mask_u8", [P, TILES, LEN], u8)
        mask_add = sb("mask_add", [P, TILES, LEN])
        ahead8 = sb("ahead8", [P, 8, 8])
        ahead4 = sb("ahead4", [P, 4, 4])
        iota_i = sb("iota_i", [P, F_EXP], i32)
        iota16 = sb("iota16", [P, F_EXP])
        eps = sb("eps", [P, 1])
        r_z = sb("r_z", [P, TILES, 16])
        r_s = sb("r_s", [P, TILES, 16])
        r_m = sb("r_m", [P, TILES, 16])
        r_big = sb("r_big", [P, 512])
        r_rank = sb("r_rank", [P, TILES, 16])
        r_a = sb("r_a", [P, 8, 4])
        r_b = sb("r_b", [P, 8, 4])
        r_c = sb("r_c", [P, 8, 4])
        r_d = sb("r_d", [P, 8, 4])
        r_max = sb("r_max", [P, TILES, 8])
        r_idx = sb("r_idx", [P, TILES, 8], u32)
        r_idf = sb("r_idf", [P, TILES, 8])
        r_sum = sb("r_sum", [P, TILES])
        r_inv = sb("r_inv", [P, TILES])
        comb = sb("comb", [P, P])
        comb_T = sb("comb_T", [P, P])
        st6 = sb("st6", [P, 2, HT, 6])
        mv = sb("mv", [P, TILES, 2])
        std = sb("std", [P, TILES])
        rstd = sb("rstd", [P, TILES])
        rp_mv = sb("rp_mv", [POSN, 2, 2])
        rp_st = sb("rp_st", [POSN, 6])
        rp_sd = sb("rp_sd", [POSN, 2])
        n2 = sb("n2", [P, TILES + 1, HEADS])
        rn = sb("rn", [P, TILES + 1, HEADS])
        k2sum = sb("k2sum", [P, TILES + 1])
        k2rn = sb("k2rn", [P, TILES + 1])
        smax = sb("smax", [P, 2, HEADS])
        ssum = sb("ssum", [P, 2, HEADS])
        p_null = sb("p_null", [P, 2, HEADS])
        g_sum = sb("g_sum", [P, TILES])

        half_neg = sb("half_neg", [P, HT])
        eps_t = sb("eps_t", [P, HT])
        var_e = sb("var_e", [P, TILES])
        with nc.sbuf_tensor("arena1", [P, 9216], f32) as arena1:
            pass
        g_hi = sb("g_hi", [P, 2, M_BLK, HW], f32r)
        g_lo = sb("g_lo", [P, 2, M_BLK, HW], f32r)
        w2b_hi = sb("w2b_hi", [P, M_FF], f32r)
        w2b_lo = sb("w2b_lo", [P, M_FF], f32r)
        g_sb = xc[:, :, :].rearrange("p t c -> p (t c)").rearrange("p (r t) -> p r t", r=2)
        g_lk = arena2[:, 1024:2048].rearrange("p (r t) -> p r t", r=2)
        early = att_bias[:, :, :, :].rearrange("p t h k -> p (t h k)")
        rp_rows = early[0:POSN, 0:5 * P].rearrange("p (n c) -> p n c", c=P)
        rp_h = early[0:POSN, 5 * P:7 * P].rearrange("p (n c) -> p n c", c=P)
        c_hid = arena1[:, 0:C_BLK * TOK].rearrange("p (b t) -> p b t", t=TOK)
        c_gate = arena1[:, C_BLK * TOK:(C_BLK + C_PAIRS) * TOK].rearrange("p (b t) -> p b t", t=TOK)
        f_hid = arena1[:, 0:F_BLK * TOK].rearrange("p (b t) -> p b t", t=TOK)
        q_T = arena1[:, 0:HB * TOK].rearrange("p (b t) -> p b t", t=TOK)
        gelu = early[:, 0:4096].rearrange("p (r b t) -> p r b t", r=2, b=M_BLK)
        late = k_diag[:, :, :, :].rearrange("p b u k -> p (b u k)")
        y_tmp = late[:, 0:1024].rearrange("p (r t) -> p r t", r=2)
        y_acc = late[:, 1024:2048].rearrange("p (s t) -> p s t", s=2)
        x_exp = f_down[:, 0:8, :].rearrange("p b c -> p (b c)").rearrange("p (r t) -> p r t", r=2)
        xh_tok = arena2[:, 6208:6464].rearrange("p (r c) -> p r c", c=P)
        xc_T = arena2[:, 6464:6720].rearrange("p (r c) -> p r c", c=P)
        w2_hi = (w_hi[:, M_EXP * M_FF:WCOLS], w2b_hi[:, :])
        w2_lo = (w_lo[:, M_EXP * M_FF:WCOLS], w2b_lo[:, :])
        f_gate = arena2[:, :].rearrange("p (b t) -> p b t", t=TOK)
        m_gate = arena2[:, :].rearrange("p (b t) -> p b t", t=TOK)
        g_tok_T = arena2[:, 0:TOK]
        xn_tok = arena2[:, 6720:6720 + TOK].rearrange("p (t c) -> p t c", c=P)
        q_sq = arena2[:, 0:2048].rearrange("p (r c) -> p r c", r=2)
        q_hat = arena2[:, 2048:4096].rearrange("p (r c) -> p r c", r=2)
        k_tok = arena2[:, 4096:4672].rearrange("p (t d) -> p t d", d=DH)
        k_sq = arena2[:, 4672:5248].rearrange("p (t d) -> p t d", d=DH)
        k_dup = arena2[:, 5248:6400].rearrange("p (t u d) -> p t u d", u=2, d=DH)
        att_T = arena2[:, 0:2048].rearrange("p (r b t) -> p r b t", r=2, b=HB)
        s_buf = arena2[:, 2048:3104].rearrange("p (r h k) -> p r h k", r=2, h=HEADS)
        e_buf = arena2[:, 3104:4160].rearrange("p (r h k) -> p r h k", r=2, h=HEADS)
        p_buf = arena2[:, 4160:5184].rearrange("p (r h k) -> p r h k", r=2, h=HEADS)
        pT_buf = arena2[:, 5184:6208].rearrange("p (r h k) -> p r h k", r=2, h=HEADS)


        ps = ctx.enter_context(nc.psum_tensor("ps", [P, 8, 512], f32))

        def bank(n):
            return ps[:, n, :]

        def split_cols(base, blocks, b):
            return lambda w: w[:, base:base + 2 * blocks * P].rearrange(
                "p (g c) -> p g c", g=2)[:, :, b * P:(b + 1) * P]

        chunks = [split_cols(C0, C_BLK, b) for b in range(C_BLK)]
        chunks += [split_cols(F0, F_BLK, b) for b in range(F_BLK)]
        chunks += [(lambda w, j=j: w[:, Q0 + j * HW:Q0 + (j + 1) * HW]) for j in range(2)]
        CH_F, CH_Q, CH_N = C_BLK, C_BLK + F_BLK, C_BLK + F_BLK + 2

        ld = {n: sem("ld_" + n) for n in (
            "x", "small", "vec", "wc", "wf", "wq", "cd", "fd", "wo", "kv", "gk", "rp", "att", "null",
            "comb_c", "gate_c0", "gate_c1", "comb_f", "gate_f0", "gate_f1", "bias_w", "bias_r", "w1", "w2",
            "gate_mw", "out")}
        m_gate_in = [sem(f"ld_gate_m{e}") for e in range(M_EXP)]
        ready = sem("pool_ready")
        pool_lo = sem("pool_lo")
        pool_mul = sem("pool_mul")
        pool_w1 = sem("pool_w1")
        pool_xe = sem("pool_xe")
        pool_acc = sem("pool_acc")
        pool_sub = sem("pool_sub")
        pool_prob = sem("pool_prob")
        pool_bias = sem("pool_bias")
        pool_chain = sem("pool_chain")
        act_chunk = sem("act_chunk")
        act_hi_s = sem("act_hi_s")
        act_exp = sem("act_exp")
        act_g = sem("act_g")
        act_rp = sem("act_rp")
        act_sqrt = sem("act_sqrt")
        act_sq = sem("act_sq")
        act_qT = sem("act_qT")
        act_pexp = sem("act_pexp")
        act_attT = sem("act_attT")
        act_w1 = sem("act_w1")
        act_w2 = sem("act_w2")
        act_pn = sem("act_pn")
        act_xcT = sem("act_xcT")
        act_xhT = sem("act_xhT")
        act_ghi = sem("act_ghi")
        pool_w2 = sem("pool_w2")
        pool_rstd = sem("pool_rstd")
        pe_xcT = sem("pe_xcT")
        v_xc = sem("v_xc")
        v_xh = sem("v_xh")
        v_st = sem("v_st")
        v_st2 = sem("v_st2")
        v_nvo = sem("v_nvo")
        v_ghi = sem("v_ghi")
        v_glo = sem("v_glo")
        v_null = sem("v_null")
        act_xe = sem("act_xe")
        act_gelu = sem("act_gelu")
        pe_small = sem("pe_small")
        pe_xT = sem("pe_xT")
        pe_log = sem("pe_log")
        pe_up = sem("pe_up")
        pe_comb = sem("pe_comb")
        pe_down = sem("pe_down")
        pe_rp = sem("pe_rp")
        pe_kv = sem("pe_kv")
        pe_kT = sem("pe_kT")
        pe_q = sem("pe_q")
        pe_qT = sem("pe_qT")
        pe_sim = sem("pe_sim")
        pe_pn = sem("pe_pn")
        pe_av = sem("pe_av")
        pe_wo = sem("pe_wo")
        pe_nv = sem("pe_nv")
        pe_m_up = sem("pe_m_up")
        pe_m_down = sem("pe_m_down")
        pe_fin = sem("pe_fin")
        v_small = sem("v_small")
        v_T = sem("v_T")
        v_lo = sem("v_lo")
        v_z = sem("v_z")
        v_comb = sem("v_comb")
        v_combT = sem("v_combT")
        v_hid = sem("v_hid")
        v_mul = sem("v_mul")
        v_rp = sem("v_rp")
        v_var = sem("v_var")
        v_xn = sem("v_xn")
        v_k = sem("v_k")
        v_kv = sem("v_kv")
        v_kd = sem("v_kd")
        v_nv = sem("v_nv")
        v_n2 = sem("v_n2")
        v_red = sem("v_red")
        v_qhat = sem("v_qhat")
        v_bias = sem("v_bias")
        v_max = sem("v_max")
        v_rs = sem("v_rs")
        v_pT = sem("v_pT")
        v_pn = sem("v_pn")
        v_wo = sem("v_wo")
        v_y = sem("v_y")
        v_out = sem("v_out")
        v_chain = sem("v_chain")

        block = ctx.enter_context(nc.Block())

        @block.sync
        def _(sp):
            for s in range(HALVES):
                sp.dma_start(x_tok[:, s * HT:(s + 1) * HT, :],
                             a["x"].rearrange("b s c -> (b s) c").rearrange("(t p) c -> p t c", p=P)
                             [:, s * HT:(s + 1) * HT, :]).then_inc(ld["x"], 16)
            sp.dma_start(wt_rows[:, :], a["L0_cond_wt"]).then_inc(ld["small"], 16)
            sp.dma_start(small_rows[0:SEQ, :], a["cond_64"]).then_inc(ld["small"], 16)
            sp.dma_start(small_rows[SEQ:SEQ + C_EXP, :], a["L0_cond_wg"]).then_inc(ld["small"], 16)
            cview = w_stage[:, C0:C0 + 2 * C_BLK * P].rearrange("p (g c) -> p g c", g=2)
            fview = w_stage[:, F0:F0 + 2 * F_BLK * P].rearrange("p (g c) -> p g c", g=2)
            for view, pre, n, s in ((cview, "L0_cond_", C_PAIRS, "wc"), (fview, "L0_ffn_", F_PAIRS, "wf")):
                for g, name in enumerate(("gate", "up")):
                    sp.dma_start(view[:, g, 0:n * P].rearrange("p (e m) -> p e m", m=DH),
                                 a[pre + "w_" + name].rearrange("e h m -> h e m")).then_inc(ld[s], 16)
                    sp.dma_start(view[:, g, n * P:(n + 1) * P], a[pre + "sw_" + name]).then_inc(ld[s], 16)
            sp.dma_start(c_down[:, 0:C_PAIRS, :], a["L0_cond_w_down"].rearrange("(q e) m c -> (e m) q c", e=2))\
                .then_inc(ld["cd"], 16)
            sp.dma_start(c_down[:, C_PAIRS, :], a["L0_cond_sw_down"]).then_inc(ld["cd"], 16)
            sp.dma_start(w_stage[:, Q0:WCOLS], a["L1_cond_Wq"]).then_inc(ld["wq"], 16)
            sp.dma_start(f_down[:, 0:F_PAIRS, :], a["L0_ffn_w_down"].rearrange("(q e) m c -> (e m) q c", e=2))\
                .then_inc(ld["fd"], 16)
            sp.dma_start(f_down[:, F_PAIRS, :], a["L0_ffn_sw_down"]).then_inc(ld["fd"], 16)
            sp.dma_start(w_kv[:, :], a["L1_cond_Wkv"]).then_inc(ld["kv"], 16)
            sp.dma_start(w_out[:, :, :], a["L1_cond_Wout"].rearrange("(b p) c -> p b c", p=P))\
                .then_inc(ld["wo"], 16)
            sp.wait_ge(v_combT, 1)
            sp.dma_start(comb_c_dram.rearrange("e (t k) -> (e t) k", k=P), comb_T[0:C_EXP * TILES, :])\
                .then_inc(ld["comb_c"], 16)
            sp.wait_ge(ld["comb_c"], 16)
            for s in range(HALVES):
                for e in range(2):
                    sp.dma_start(c_gate[e * DH:(e + 1) * DH, :, s * HW:(s + 1) * HW],
                                 comb_c_dram.rearrange("(q e) k -> e q k", e=2)[e, :, s * HW:(s + 1) * HW]
                                 .partition_broadcast(DH)).then_inc(ld[f"gate_c{s}"], 16)
            sp.wait_ge(v_combT, 2)
            sp.dma_start(comb_f_dram.rearrange("e (t k) -> (e t) k", k=P), comb_T[:, :])\
                .then_inc(ld["comb_f"], 16)
            sp.wait_ge(ld["comb_f"], 16)
            for s in range(HALVES):
                for e in range(2):
                    sp.dma_start(f_gate[e * DH:(e + 1) * DH, :, s * HW:(s + 1) * HW],
                                 comb_f_dram.rearrange("(q e) k -> e q k", e=2)[e, :, s * HW:(s + 1) * HW]
                                 .partition_broadcast(DH)).then_inc(ld[f"gate_f{s}"], 16)
            sp.wait_ge(v_rp, 8)
            row = rp_out[:, 0:LEN]
            skew = bass.AP(row.tensor, row.offset + LEN - 1, [list(row.ap[0]), [-1, LEN], [1, LEN]])
            sp.dma_start(bias_dram, skew).then_inc(ld["bias_w"], 16)
            sp.wait_ge(ld["bias_w"], 16)
            for s in range(BPT):
                sp.dma_start(base_bias[s * LEN:(s + 1) * LEN, :, :], bias_dram.rearrange("h i j -> i h j")).then_inc(ld["bias_r"], 16)
            sp.wait_ge(pool_lo, CH_N)
            sp.wait_ge(act_chunk, CH_N)
            w1_stage = w_stage[:, 0:M_EXP * M_FF].rearrange("p (e f) -> p e f", f=M_FF)
            sp.dma_start(w1_stage, a["L1_ffn_W1"].rearrange("e h f -> h e f")).then_inc(ld["w1"], 16)
            sp.wait_ge(pe_down, 4)
            sp.dma_start(k_tok[:, TILES, :], a["cond_64"][0, :].partition_broadcast(P)).then_inc(ld["null"], 16)
            sp.wait_ge(pool_w1, M_EXP)
            sp.wait_ge(act_w1, M_EXP)
            w2_stage = w_stage[:, 0:M_EXP * M_FF].rearrange("p (e b c) -> p e b c", e=M_EXP, c=P)
            for e in range(M_EXP):
                sp.dma_start(w2_stage[:, e], a["L1_ffn_W2"][e].rearrange("(b p) c -> p b c", p=P))\
                    .then_inc(ld["w2"], 16)
            sp.wait_ge(v_combT, 3)
            sp.dma_start(gate_m_dram.rearrange("e (t k) -> (e t) k", k=P), comb_T[0:M_EXP * TILES, :])\
                .then_inc(ld["gate_mw"], 16)
            sp.wait_ge(ld["gate_mw"], 16)
            for e in range(M_EXP):
                sp.dma_start(m_gate[:, e, :], gate_m_dram[e].partition_broadcast(P)).then_inc(m_gate_in[e], 16)
            for s in range(HALVES):
                sp.wait_ge(v_out, s + 1)
                sp.dma_start(out.rearrange("b s c -> (b s) c").rearrange("(t p) c -> p t c", p=P)
                             [:, s * HT:(s + 1) * HT, :], x_tok[:, s * HT:(s + 1) * HT, :])\
                    .then_inc(ld["out"], 16)
            sp.wait_ge(ld["out"], 32)

        @block.gpsimd
        def _(pool):
            n_chain = [0]

            def link(ins):
                n_chain[0] += 1
                ins.then_inc(pool_chain, 1)
                pool.wait_ge(pool_chain, n_chain[0])

            link(pool.memset(ident[:, :], 0.0))
            pool.affine_select(out=ident[:, :], in_=ident[:, :], compare_op=ALU.not_equal, fill=1.0, base=0,
                               pattern=[[-1, P]], channel_multiplier=1).then_inc(ready, 1)
            pool.memset(g_tok_T, 0.0).then_inc(ready, 1)
            link(pool.memset(gk[:, :], 0.0))
            link(pool.memset(router_w[:, :], 0.0))
            pool.memset(half_neg[:, :], -0.5)
            link(pool.memset(eps_t[:, :], LN_EPS))
            for t, n in ((ahead8, 8), (ahead4, 4)):
                link(pool.memset(t[:, :, :], 0.0))
                pool.affine_select(out=t[:, :, :], in_=t[:, :, :], compare_op=ALU.is_gt, fill=TINY, base=0,
                                   pattern=[[1, n], [-1, n]], channel_multiplier=0).then_inc(ready, 1)
            for t, name, rows in ((0, "L1_ffn_ln_g", 8), (8, "L1_ffn_ln_b", 8), (48, "L1_ffn_b2", 8)):
                pool.dma_start(vec_rows[t:t + rows, :], a[name]).then_inc(ld["vec"], 16)
            pool.dma_start(vec_rows[V_B1:V_B2, :], a["L1_ffn_b1"].rearrange("e (b p) -> (e b) p", p=P))\
                .then_inc(ld["vec"], 16)
            pool.dma_start(vec_rows[V_GN:V_ROWS, :], a["L1_cond_g_norm"].unsqueeze(0)).then_inc(ld["vec"], 16)
            pool.iota(pos_i[:, :], pattern=[[0, 1]], base=LEN - 1, channel_multiplier=-1).then_inc(ready, 1)
            pool.iota(iota_i[:, :], pattern=[[1, F_EXP]], base=0, channel_multiplier=0).then_inc(ready, 1)
            for n, name in enumerate(("w0", "b0", "g0", "b1", "g1")):
                src = a["L1_cond_" + name]
                src = src[0, :] if name == "w0" else src
                pool.dma_start(rp_rows[:, n, :], src.partition_broadcast(POSN)).then_inc(ld["rp"], 16)
            pool.dma_start(rp_w1[:, :], a["L1_cond_w1"]).then_inc(ld["rp"], 16)
            pool.dma_start(rp_w2[:, :], a["L1_cond_w2"]).then_inc(ld["rp"], 16)
            pool.dma_start(rp_b2[:, :], a["L1_cond_b2"].unsqueeze(1)).then_inc(ld["rp"], 16)
            pool.dma_start(gk[:, 0:F_EXP], a["L0_ffn_gate_kernel"]).then_inc(ld["gk"], 16)
            pool.dma_start(f_bias[:, :], a["L0_ffn_gate_bias"].partition_broadcast(P)).then_inc(ld["gk"], 16)
            pool.dma_start(router_w[:, 0:M_EXP], a["L1_ffn_router_W"]).then_inc(ld["gk"], 16)
            pool.dma_start(router_b[:, :], a["L1_ffn_router_b"].partition_broadcast(P)).then_inc(ld["gk"], 16)
            for n, name in enumerate(("q_scale", "k_scale")):
                pool.dma_start(qk_scale[:, n, :], a["L1_cond_" + name].partition_broadcast(P))\
                    .then_inc(ld["att"], 16)
            pool.dma_start(null_b[:, :], a["L1_cond_null_attn_bias"].partition_broadcast(P)).then_inc(ld["att"], 16)
            pool.dma_start(g_out[:, :], a["L1_cond_g_out"].partition_broadcast(P)).then_inc(ld["att"], 16)
            for s in range(BPT):
                pool.dma_start(mask_u8[s * LEN:(s + 1) * LEN, :, :],
                               a["mask_BxS_bf1"].rearrange("(t s) j -> s t j", s=BPT)[s].partition_broadcast(LEN))\
                    .then_inc(ld["att"], 16)
            for h in range(2):
                pool.dma_start(nv_col[h * DH:(h + 1) * DH, :], a["cond_64"][1, :].unsqueeze(1))\
                    .then_inc(ld["att"], 16)

            def split(n):
                pool.wait_ge(act_chunk, n + 1)
                c = chunks[n]
                pool.tensor_tensor(c(w_lo), c(w_stage), c(w_hi).bitcast(f32), ALU.subtract).then_inc(pool_lo, 1)

            for n in range(CH_N):
                split(n)
                if n == C_BLK:
                    pool.memset(k_diag[:, :, :, :], 0.0).then_inc(ready, 1)
                    pool.memset(v_diag[:, :, :, :], 0.0).then_inc(ready, 1)
                    pool.memset(nv_sel[:, :, :], 0.0).then_inc(ready, 1)
                    pool.memset(nv_out[:, :], 0.0).then_inc(ready, 1)
                    pool.memset(pn_T[:, :], 0.0).then_inc(ready, 1)

            for s in range(HALVES):
                pool.wait_ge(ld[f"gate_c{s}"], 32)
                cols = slice(s * HW, (s + 1) * HW)
                for q in (3,):
                    pool.wait_ge(v_hid, C_BLK * s + q + 1)
                    pool.tensor_tensor(c_hid[:, q, cols], c_hid[:, q, cols], c_gate[:, q, cols], ALU.mult)\
                        .then_inc(pool_mul, 1)

            for s in range(HALVES):
                cols = slice(s * HW, (s + 1) * HW)
                pool.wait_ge(ld[f"gate_f{s}"], 32)
                for q in (5, 6, 7):
                    pool.wait_ge(v_hid, 2 * C_BLK + F_BLK * s + q + 1)
                    pool.tensor_tensor(f_hid[:, q, cols], f_hid[:, q, cols], f_gate[:, q, cols], ALU.mult)\
                        .then_inc(pool_mul, 1)

            pool.wait_ge(ld["bias_r"], 16 * BPT)
            for s in range(BPT):
                b = base_bias[s * LEN:(s + 1) * LEN, :, :]
                pool.affine_select(out=b, in_=b, compare_op=ALU.is_ge, fill=MASKED, base=0,
                                   pattern=[[0, HEADS], [-1, LEN]], channel_multiplier=1).then_inc(pool_bias, 1)
                pool.wait_ge(pool_bias, s + 1)

            def rstd_of(n, cols):
                m = cols.stop - cols.start
                link(pool.tensor_tensor(var_e[:, cols], mv[:, cols, 1], eps_t[:, 0:m], ALU.add))
                pool.tensor_tensor(rstd[:, cols], var_e[:, cols], half_neg[:, 0:m], ALU.pow).then_inc(pool_rstd, 1)

            for s in range(HALVES):
                pool.wait_ge(v_var, s + 1)
                rstd_of(s, slice(s * HT, (s + 1) * HT))

            def subtract(t):
                pool.wait_ge(v_max, t + 1)
                pool.tensor_tensor(s_buf[:, t % 2], s_buf[:, t % 2],
                                   smax[:, t % 2, :].unsqueeze(2).broadcast_to([P, HEADS, KEYS]), ALU.subtract)\
                    .then_inc(pool_sub, 1)

            def probs(t):
                pool.wait_ge(v_rs, t + 1)
                if t >= 2:
                    pool.wait_ge(v_pT, t - 1)
                pool.tensor_tensor(p_buf[:, t % 2], e_buf[:, t % 2, :, 0:LEN],
                                   ssum[:, t % 2, :].unsqueeze(2).broadcast_to([P, HEADS, LEN]), ALU.mult)\
                    .then_inc(pool_prob, 1)

            def split_w1(e):
                pool.wait_ge(act_w1, e + 1)
                c = slice(e * M_FF, (e + 1) * M_FF)
                pool.tensor_tensor(w_lo[:, c], w_stage[:, c], w_hi[:, c].bitcast(f32), ALU.subtract)\
                    .then_inc(pool_w1, 1)

            def norms(t):
                pool.wait_ge(v_st, t + 1)
                rstd_of(0, slice(t, t + 1))
                pool.wait_ge(v_st2, t + 1)
                rstd_of(0, slice(t, t + 1))

            subtract(0)
            subtract(1)
            probs(0)
            for t in range(TILES):
                if t + 1 < TILES:
                    probs(t + 1)
                if t >= 1:
                    norms(t - 1)
                split_w1(t)
                if t + 2 < TILES:
                    subtract(t + 2)

            def low_input(k):
                pool.wait_ge(act_xe, 2 * (k + 1))
                if k >= 2:
                    pool.wait_ge(pe_m_up, M_BLK * (k - 1))
                pool.tensor_tensor(act_lo[:, (k % 2) * HW:(k % 2 + 1) * HW], x_exp[:, k % 2],
                                   act_hi[:, (k % 2) * HW:(k % 2 + 1) * HW].bitcast(f32), ALU.subtract)\
                    .then_inc(pool_xe, 1)

            def split_w2(e):
                pool.wait_ge(act_w2, e + 1)
                pool.tensor_tensor(w2_lo[e % 2], w_stage[:, e * M_FF:(e + 1) * M_FF], w2_hi[e % 2].bitcast(f32),
                                   ALU.subtract).then_inc(pool_w2, 1)

            low_input(0)
            norms(TILES - 1)
            steps = M_EXP * HALVES
            for k in range(1, steps + 3):
                if k < steps:
                    low_input(k)
                if k % 2 and k // 2 < M_EXP:
                    split_w2(k // 2)
                if k >= 3:
                    j = k - 3
                    pool.wait_ge(v_y, j + 1)
                    if j >= 2:
                        pool.wait_ge(pool_acc, j)
                        pool.tensor_tensor(y_acc[:, j % 2], y_acc[:, j % 2], y_tmp[:, j % 2], ALU.add)\
                            .then_inc(pool_acc, 1)
                    else:
                        pool.tensor_copy(y_acc[:, j % 2], y_tmp[:, j % 2]).then_inc(pool_acc, 1)

        @block.scalar
        def _(act):
            def copy_hi(n):
                act.wait_ge(v_T, n + 1)
                cols = slice(n % 2 * HW, (n % 2 + 1) * HW)
                act.activation(act_hi[:, cols], act_T[:, cols], ACT.Copy).then_inc(act_hi_s, 1)

            def chunk(n):
                act.wait_ge(ld["wc" if n < CH_F else "wf" if n < CH_Q else "wq"], 64 if n < CH_Q else 16)
                act.activation(chunks[n](w_hi), chunks[n](w_stage), ACT.Copy).then_inc(act_chunk, 1)

            chunk(0)
            for s in range(HALVES):
                copy_hi(s)
            for n in range(1, CH_F):
                chunk(n)
            act.wait_ge(v_z, 1)
            act.activation(r_s[:, :, 0:C_EXP], r_z[:, :, 0:C_EXP], ACT.Exp).then_inc(act_exp, 1)

            def gate_copy(u):
                act.wait_ge(pe_up, u + 1)
                if u >= 2:
                    act.wait_ge(v_hid, u - 1)
                act.activation(g_sb[:, u % 2], bank(2 * (u % 2)), ACT.Copy).then_inc(act_g, 1)

            for u in range(2 * C_BLK):
                gate_copy(u)
                if CH_F + u < CH_N:
                    chunk(CH_F + u)
                if u == 5:
                    act.wait_ge(v_rp, 1)
                    act.activation(rp_sd[:, 0:1], rp_mv[:, 0, 1:2], ACT.Sqrt, bias=eps[0:POSN, :])\
                        .then_inc(act_rp, 1)
            chunk(CH_F + 10)
            for s in range(HALVES):
                copy_hi(2 + s)
            act.wait_ge(pe_log, 2)
            act.activation(r_s[:, :, :], bank(4)[:, 0:P].rearrange("p (t e) -> p t e", e=F_EXP), ACT.Sigmoid)\
                .then_inc(act_exp, 1)
            act.wait_ge(v_rp, 2)
            act.activation(rp_h[:, 1, :], rp_h[:, 0, :], ACT.Silu).then_inc(act_rp, 1)
            for u in range(2 * C_BLK, 2 * C_BLK + 2 * F_BLK):
                act.wait_ge(pe_up, u + 1)
                act.wait_ge(v_hid, u - 1)
                act.activation(g_sb[:, u % 2], bank(2 * (u % 2)), ACT.Silu).then_inc(act_g, 1)
                if u == 2 * C_BLK + 6:
                    act.wait_ge(v_rp, 4)
                    act.activation(rp_sd[:, 1:2], rp_mv[:, 1, 1:2], ACT.Sqrt, bias=eps[0:POSN, :])\
                        .then_inc(act_rp, 1)
                if u == 2 * C_BLK + 8:
                    act.wait_ge(v_rp, 5)
                    act.activation(rp_h[:, 1, :], rp_h[:, 0, :], ACT.Silu).then_inc(act_rp, 1)

            copy_hi(4)

            def q_squares(t):
                act.wait_ge(pe_q, t + 1)
                if t >= 2:
                    act.wait_ge(v_red, t - 1)
                act.activation(q_sq[:, t % 2, :], ps[:, 2 * (t % 2):2 * (t % 2) + 2, :].rearrange("p b c -> p (b c)"),
                               ACT.Square).then_inc(act_sq, 1)
                if t == 0:
                    copy_hi(5)
                act.wait_ge(v_red, t + 1)
                act.activation(rn[:, t, :], n2[:, t, :], ACT.Sqrt).then_inc(act_sqrt, 1)

            def q_turned(t):
                act.wait_ge(pe_qT, t + 1)
                act.activation(q_T[:, :, t * P:(t + 1) * P],
                               ps[:, 4 + 2 * (t % 2):6 + 2 * (t % 2), :].rearrange("p b (c k) -> p (b c) k", k=P),
                               ACT.Copy).then_inc(act_qT, 1)

            for t in range(TILES):
                q_squares(t)
                if t == 2:
                    act.wait_ge(v_n2, 1)
                    act.activation(k2rn[:, :], k2sum[:, :], ACT.Sqrt).then_inc(act_sqrt, 1)
                if t >= 1:
                    q_turned(t - 1)
            q_turned(TILES - 1)

            def att_turned(t):
                act.wait_ge(pe_av, t + 1)
                if t >= 2:
                    act.wait_ge(pe_wo, t - 1)
                act.activation(att_T[:, t % 2].rearrange("p b (s i) -> p b s i", s=BPT),
                               ps[:, 4:6, :].rearrange("p h (s b i) -> p b (h s) i", s=2, b=HB),
                               ACT.Copy).then_inc(act_attT, 1)

            def high_w1(e):
                act.wait_ge(ld["w1"], 16)
                c = slice(e * M_FF, (e + 1) * M_FF)
                act.activation(w_hi[:, c], w_stage[:, c], ACT.Copy).then_inc(act_w1, 1)

            def exps(t):
                act.wait_ge(pool_sub, t + 1)
                if t >= 2:
                    act.wait_ge(pool_prob, t - 1)
                    act.wait_ge(v_pn, t - 1)
                act.activation(e_buf[:, t % 2], s_buf[:, t % 2], ACT.Exp).then_inc(act_pexp, 1)

            def null_turned(t):
                act.wait_ge(pe_pn, t + 1)
                if t >= 1:
                    act.wait_ge(pe_wo, t)
                act.activation(pn_T[0:HEADS, :], bank(7)[0:HEADS, 0:P], ACT.Copy).then_inc(act_pn, 1)

            def out_turned(t):
                act.wait_ge(pe_xcT, t + 1)
                if t >= 2:
                    act.wait_ge(pe_log, 2 + t - 1)
                act.activation(xc_T[:, t % 2, :], bank(7)[:, 0:P], ACT.Copy).then_inc(act_xcT, 1)
                act.activation(act_T[:, t * P:(t + 1) * P], bank(7)[:, P:2 * P], ACT.Copy).then_inc(act_xhT, 1)

            def expert_input(k):
                e, s = divmod(k, HALVES)
                act.wait_ge(act_xhT, TILES if s else HT)
                if k >= 2:
                    act.wait_ge(pool_xe, k - 1)
                act.activation(x_exp[:, k % 2], act_T[:, s * HW:(s + 1) * HW], ACT.Identity,
                               scale=vec[:, V_LNG + e:V_LNG + e + 1], bias=vec[:, V_LNB + e:V_LNB + e + 1])\
                    .then_inc(act_xe, 1)
                if k >= 2:
                    act.wait_ge(pe_m_up, M_BLK * (k - 1))
                act.wait_ge(act_xe, 2 * k + 1)
                act.activation(act_hi[:, (k % 2) * HW:(k % 2 + 1) * HW], x_exp[:, k % 2], ACT.Copy)\
                    .then_inc(act_xe, 1)

            exps(0)
            exps(1)
            for t in range(TILES):
                null_turned(t)
                high_w1(t)
                att_turned(t)
                if t >= 1:
                    out_turned(t - 1)
                if t + 2 < TILES:
                    exps(t + 2)
            expert_input(0)
            out_turned(TILES - 1)

            def high_w2(e):
                act.wait_ge(ld["w2"], 16 * M_EXP)
                if e >= 2:
                    act.wait_ge(pe_m_down, 2 * (e - 1))
                act.activation(w2_hi[e % 2], w_stage[:, e * M_FF:(e + 1) * M_FF], ACT.Copy).then_inc(act_w2, 1)

            steps = M_EXP * HALVES
            expert_input(1)
            for k in range(steps):
                e = k // HALVES
                if k == 1:
                    act.wait_ge(v_z, 2)
                    act.activation(r_s[:, :, 0:M_EXP], r_z[:, :, 0:M_EXP], ACT.Exp).then_inc(act_exp, 1)
                if k % 2 == 0:
                    high_w2(e)
                for b in range(M_BLK):
                    act.wait_ge(pe_m_up, M_BLK * k + b + 1)
                    if k >= 2:
                        act.wait_ge(v_glo, 2 * (k - 2) + b // 2 + 1)
                    c = V_B1 + e * M_BLK + b
                    act.activation(gelu[:, k % 2, b, :], bank(b), ACT.Gelu, bias=vec[:, c:c + 1])\
                        .then_inc(act_gelu, 1)
                act.wait_ge(act_gelu, M_BLK * (k + 1))
                if k >= 2:
                    act.wait_ge(pe_m_down, k - 1)
                act.activation(g_hi[:, k % 2, 2:4, :], gelu[:, k % 2, 2:4, :], ACT.Copy).then_inc(act_ghi, 1)
                if k + 2 < steps:
                    expert_input(k + 2)

        @block.tensor
        def _(pe):
            def three(dst, w, x, n=1, first=True, last=True):
                (wh, wl), (xh, xl) = w, x
                pe.matmul(dst, wh, xh, start=first, stop=False)
                pe.matmul(dst, wh, xl, start=False, stop=False)
                return pe.matmul(dst, wl, xh, start=False, stop=last)

            def half_pair(s):
                return act_hi[:, s * HW:(s + 1) * HW], act_lo[:, s * HW:(s + 1) * HW]

            pe.wait_ge(ready, 1)
            pe.wait_ge(ld["small"], 48)
            pe.transpose(bank(7)[:, 0:C_EXP], wt_rows[:, :], ident[0:C_EXP, 0:C_EXP])
            pe.transpose(bank(7)[0:DH, 64:64 + SEQ + C_EXP], small_rows[:, :],
                         ident[0:SEQ + C_EXP, 0:SEQ + C_EXP]).then_inc(pe_small, 1)
            for s in range(HALVES):
                pe.wait_ge(ld["x"], 32)
                for t in range(HT):
                    mm = pe.transpose(bank(4 + s)[:, t * P:(t + 1) * P], x_tok[:, s * HT + t, :], ident[:, :])
                mm.then_inc(pe_xT, 1)
            pe.wait_ge(v_small, 3)
            for t in range(TILES):
                pe.wait_ge(v_T, t // HT + 1)
                o = bank(6)[:, t * C_EXP:t * C_EXP + PAD]
                pe.matmul(o, act_T[:, t * P:(t + 1) * P], wt_T[:, :], start=True, stop=False)
                mm = pe.matmul(o, g_tok_T[:, t * P:(t + 1) * P], wg_T[:, :], start=False, stop=True)
            mm.then_inc(pe_log, 1)

            def up_unit(u, base, blocks, s, b, hi_need, lo_need, ch):
                pe.wait_ge(act_hi_s, hi_need)
                pe.wait_ge(v_lo, lo_need)
                pe.wait_ge(pool_lo, ch)
                if u >= 2:
                    pe.wait_ge(act_g, u - 1)
                    pe.wait_ge(v_hid, u - 1)
                for g in range(2):
                    c = slice(base + (g * blocks + b) * P, base + (g * blocks + b + 1) * P)
                    mm = three(bank(2 * (u % 2) + g), (w_hi[:, c], w_lo[:, c]), half_pair(s))
                mm.then_inc(pe_up, 1)

            def turn_gates(n, rows):
                pe.wait_ge(v_comb, n)
                pe.transpose(bank(5)[0:rows, 0:P], comb[:, 0:rows], ident[:, :]).then_inc(pe_comb, 1)

            def rel_turn(n):
                pe.wait_ge(act_rp, 2 * n)
                pe.transpose(bank(7)[:, 256:256 + POSN], rp_h[:, 1, :], ident[0:POSN, 0:POSN]).then_inc(pe_rp, 1)

            for u in range(2 * C_BLK):
                s, b = divmod(u, C_BLK)
                up_unit(u, C0, C_BLK, s, b, s + 1, s + 1, b + 1)
                if u == 5:
                    pe.wait_ge(ld["vec"], 80)
                    pe.transpose(bank(7)[:, 128:128 + V_ROWS], vec_rows[:, :], ident[0:V_ROWS, 0:V_ROWS])\
                        .then_inc(pe_small, 1)
                if u == 6:
                    turn_gates(1, C_EXP * TILES)
            pe.wait_ge(ld["cd"], 32)
            for s in range(HALVES):
                if s == 1:
                    pe.wait_ge(v_small, 4)
                order = (C_PAIRS, 0, 1, 2, 3)
                for n, b in enumerate(order):
                    if b == C_PAIRS:
                        pe.wait_ge(v_hid, C_BLK * (s + 1))
                    if b == 0:
                        pe.wait_ge(v_mul, s + 1)
                    if b == 3:
                        pe.wait_ge(pool_mul, s + 1)
                    mm = pe.matmul(bank(6 + s), c_down[:, b, :], c_hid[:, b, s * HW:(s + 1) * HW],
                                   start=(n == 0), stop=(n == C_BLK - 1))
                mm.then_inc(pe_down, 1)
            pe.wait_ge(ld["gk"], 64)
            for t in range(TILES):
                pe.wait_ge(v_T, 2 + t // HT + 1)
                mm = pe.matmul(bank(4)[:, t * F_EXP:t * F_EXP + PAD], act_T[:, t * P:(t + 1) * P], gk[:, :],
                               start=True, stop=True)
            mm.then_inc(pe_log, 1)
            for j in range(2 * F_BLK):
                u = 2 * C_BLK + j
                s, b = divmod(j, F_BLK)
                up_unit(u, F0, F_BLK, s, b, 2 + s + 1, 2 + s + 1, CH_F + b + 1)
                if j == 1:
                    rel_turn(1)
                if j == 3:
                    pe.wait_ge(v_rp, 3)
                    pe.matmul(bank(7)[0:POSN, 320:448], rp_T[:, 0, :], rp_w1[:, :], start=True, stop=True)\
                        .then_inc(pe_rp, 1)
                if j == 9:
                    rel_turn(2)
                if j == 12:
                    pe.wait_ge(v_rp, 6)
                    pe.matmul(bank(7)[0:HEADS, 320:320 + POSN], rp_w2[:, :], rp_T[:, 1, :], start=True, stop=True)\
                        .then_inc(pe_rp, 1)
                if j == 10:
                    turn_gates(2, P)
            def turn_tiles(s):
                pe.wait_ge(v_xn, s + 1)
                for t in range(HT):
                    mm = pe.transpose(bank(4 + s)[:, t * P:(t + 1) * P], xn_tok[:, s * HT + t, :], ident[:, :])
                mm.then_inc(pe_xT, 1)

            pe.wait_ge(ld["fd"], 32)
            pe.wait_ge(v_rp, 8)
            for s in range(HALVES):
                pe.wait_ge(v_hid, 2 * C_BLK + F_BLK * (s + 1))
                pe.wait_ge(v_mul, 2 + s + 1)
                pe.wait_ge(pool_mul, 2 + 3 * (s + 1))
                for t in range(HT):
                    if s == 1 and t == 3:
                        turn_tiles(0)
                    cols = slice((s * HT + t) * P, (s * HT + t + 1) * P)
                    for b in range(F_BLK):
                        mm = pe.matmul(bank(6 + s)[:, t * P:(t + 1) * P], f_hid[:, b, cols], f_down[:, b, :],
                                       start=(b == 0), stop=(b == F_BLK - 1))
                mm.then_inc(pe_down, 1)
            pe.wait_ge(v_nv, 1)
            pe.wait_ge(ld["wo"], 16)
            for b in range(HB):
                mm = pe.matmul(bank(3)[0:HEADS, 0:P], nv_sel[:, b, :], w_out[:, b, :],
                               start=(b == 0), stop=(b == HB - 1))
            mm.then_inc(pe_nv, 1)
            def kv_rows(s):
                pe.wait_ge(ld["kv"], 16)
                pe.wait_ge(v_T, 4 + s + 1)
                for t in range(HT):
                    cols = slice((s * HT + t) * P, (s * HT + t + 1) * P)
                    mm = pe.matmul(bank(6 + s)[:, t * P:(t + 1) * P], act_T[:, cols], w_kv[:, :],
                                   start=True, stop=True)
                mm.then_inc(pe_kv, 1)

            def q_rows(t):
                pe.wait_ge(act_hi_s, 4 + t // HT + 1)
                pe.wait_ge(v_lo, 4 + t // HT + 1)
                pe.wait_ge(pool_lo, CH_N)
                if t == 1:
                    pe.wait_ge(v_nvo, 1)
                if t >= 2:
                    pe.wait_ge(v_qhat, t - 1)
                cols = slice(t * P, (t + 1) * P)
                for j in range(2):
                    c = slice(Q0 + j * HW, Q0 + (j + 1) * HW)
                    mm = three(bank(2 * (t % 2) + j), (act_hi[:, cols], act_lo[:, cols]), (w_hi[:, c], w_lo[:, c]))
                mm.then_inc(pe_q, 1)

            def q_turn(t):
                pe.wait_ge(v_qhat, t + 1)
                if t == 0:
                    pe.wait_ge(v_T, 5)
                if t == 1:
                    pe.wait_ge(v_kv, 1)
                if t >= 2:
                    pe.wait_ge(act_qT, t - 1)
                for b in range(HB):
                    mm = pe.transpose(bank(4 + 2 * (t % 2) + b // 4)[:, (b % 4) * P:(b % 4 + 1) * P],
                                      q_hat[:, t % 2, b * P:(b + 1) * P], ident[:, :])
                mm.then_inc(pe_qT, 1)

            kv_rows(0)
            q_rows(0)
            turn_tiles(1)
            q_rows(1)
            kv_rows(1)
            for t in range(TILES):
                if t == 0:
                    pe.wait_ge(v_T, 6)
                q_turn(t)
                if t + 2 < TILES:
                    q_rows(t + 2)
            pe.wait_ge(v_k, 1)
            pe.wait_ge(v_qhat, TILES)
            for t in range(TILES + 1):
                mm = pe.transpose(bank(t // HT)[:, (t % HT) * P:(t % HT + 1) * P],
                                  k_dup[:, t].rearrange("p u d -> p (u d)"), ident[:, :])
            mm.then_inc(pe_kT, 1)

            def scores(t):
                pe.wait_ge(act_qT, TILES)
                if t >= 2:
                    pe.wait_ge(v_max, t - 1)
                pe.wait_ge(v_kd, 1)
                for b in range(HB):
                    for s in range(BPT):
                        mm = pe.matmul(ps[s * LEN:(s + 1) * LEN, 2 * (t % 2) + b // 4,
                                          (b % 4) * 2 * KEYS:(b % 4 + 1) * 2 * KEYS],
                                       q_T[:, b, t * P + s * LEN:t * P + (s + 1) * LEN],
                                       k_diag[:, t * BPT + s].rearrange("p u k -> p (u k)"), start=True, stop=True)
                mm.then_inc(pe_sim, 1)

            def null_turn(t):
                pe.wait_ge(v_pn, t + 1)
                if t >= 2:
                    pe.wait_ge(act_xhT, t - 1)
                pe.transpose(bank(7)[0:HEADS, 0:P], p_null[:, t % 2, :], ident[:, :]).then_inc(pe_pn, 1)

            def out_turn(t):
                pe.wait_ge(act_pn, min(t + 2, TILES))
                pe.wait_ge(v_xc, t + 1)
                pe.transpose(bank(7)[:, 0:P], xc[:, t, :], ident[:, :])
                pe.wait_ge(v_xh, t + 1)
                pe.transpose(bank(7)[:, P:2 * P], xh_tok[:, t % 2, :], ident[:, :]).then_inc(pe_xcT, 1)

            def route(t):
                pe.wait_ge(act_xhT, t + 1)
                pe.wait_ge(act_pn, min(t + 3, TILES))
                pe.matmul(bank(7)[:, 256 + t * M_EXP:256 + t * M_EXP + PAD], xc_T[:, t % 2, :], router_w[:, :],
                          start=True, stop=True).then_inc(pe_log, 1)

            def values(t):
                pe.wait_ge(v_pT, t + 1)
                if t >= 1:
                    pe.wait_ge(act_attT, t)
                for s in range(BPT):
                    for h in range(2):
                        mm = pe.matmul(ps[h * DH:(h + 1) * DH, 4 + s // 2,
                                          (s % 2) * HB * LEN:(s % 2 + 1) * HB * LEN],
                                       v_diag[:, t, s, :],
                                       pT_buf[:, t % 2].rearrange("p (b u) i -> p u b i", u=2)[:, h],
                                       start=True, stop=True)
                mm.then_inc(pe_av, 1)

            def project(t):
                pe.wait_ge(act_attT, t + 1)
                pe.wait_ge(act_pn, t + 1)
                if t >= 1:
                    pe.wait_ge(v_wo, t)
                for b in range(HB):
                    pe.matmul(bank(6)[:, 0:P], att_T[:, t % 2, b, :], w_out[:, b, :], start=(b == 0), stop=False)
                pe.matmul(bank(6)[:, 0:P], pn_T[:, :], nv_out[:, :], start=False, stop=True).then_inc(pe_wo, 1)

            scores(0)
            scores(1)
            for t in range(TILES):
                null_turn(t)
                values(t)
                if t + 2 < TILES:
                    scores(t + 2)
                if t >= 2:
                    route(t - 2)
                project(t)
                if t >= 1:
                    out_turn(t - 1)

            def m_up(k):
                e = k // HALVES
                pe.wait_ge(pool_xe, k + 1)
                r = k % 2
                x = act_hi[:, r * HW:(r + 1) * HW], act_lo[:, r * HW:(r + 1) * HW]
                for b in range(M_BLK):
                    if k >= 1:
                        pe.wait_ge(act_gelu, M_BLK * (k - 1) + b + 1)
                    if k == 0:
                        pe.wait_ge(v_max, TILES)
                    c = slice(e * M_FF + b * P, e * M_FF + (b + 1) * P)
                    three(bank(b), (w_hi[:, c], w_lo[:, c]), x).then_inc(pe_m_up, 1)

            def m_down(k):
                e = k // HALVES
                pe.wait_ge(pool_w2, e + 1)
                if k == 0:
                    pe.wait_ge(v_wo, TILES)
                if k == 1:
                    pe.wait_ge(v_comb, 3)
                if k >= 2:
                    pe.wait_ge(v_y, k - 1)
                for b in range(M_BLK):
                    pe.wait_ge(v_glo, 2 * k + b // 2 + 1)
                    c = slice(b * P, (b + 1) * P)
                    mm = three(bank(6 + k % 2), (w2_hi[e % 2][:, c], w2_lo[e % 2][:, c]),
                               (g_hi[:, k % 2, b, :], g_lo[:, k % 2, b, :]), first=(b == 0), last=(b == M_BLK - 1))
                mm.then_inc(pe_m_down, 1)

            steps = M_EXP * HALVES
            m_up(0)
            route(TILES - 2)
            out_turn(TILES - 1)
            for k in range(steps):
                if k + 1 < steps:
                    m_up(k + 1)
                if k == 0:
                    route(TILES - 1)
                if k == 1:
                    turn_gates(3, M_EXP * TILES)
                m_down(k)
            pe.wait_ge(v_combT, 3)
            for s in range(HALVES):
                pe.wait_ge(pool_acc, steps - 1 + s)
                for t in range(HT):
                    mm = pe.transpose(bank(4 + s)[:, t * P:(t + 1) * P], y_acc[:, s, t * P:(t + 1) * P], ident[:, :])
                mm.then_inc(pe_fin, 1)

        @block.vector
        def _(dve):
            n_chain = [0]

            def link(ins):
                n_chain[0] += 1
                ins.then_inc(v_chain, 1)
                dve.wait_ge(v_chain, n_chain[0])

            def turned(s, src, base, scale=None, lo=True):
                cols = slice(s * HW, (s + 1) * HW)
                if scale is None:
                    dve.tensor_copy(act_T[:, cols], src).then_inc(v_T, 1)
                else:
                    dve.tensor_scalar(act_T[:, cols], src, scale, None, ALU.mult).then_inc(v_T, 1)
                if lo:
                    dve.wait_ge(v_T, base + s + 1)
                    dve.wait_ge(act_hi_s, base + s + 1)
                    dve.tensor_tensor(act_lo[:, cols], act_T[:, cols], act_hi[:, cols].bitcast(f32), ALU.subtract)\
                        .then_inc(v_lo, 1)

            link(dve.memset(eps[:, :], LN_EPS))
            link(dve.memset(wt_T[:, :], 0.0))
            link(dve.memset(wg_T[:, :], 0.0))
            dve.wait_ge(pe_small, 1)
            dve.wait_ge(ready, 2)
            dve.tensor_copy(wt_T[:, 0:C_EXP], bank(7)[:, 0:C_EXP]).then_inc(v_small, 1)
            dve.tensor_copy(g_tok_T[0:DH, :].rearrange("p (b i) -> p b i", i=LEN),
                            bank(7)[0:DH, 64:64 + SEQ].unsqueeze(2).broadcast_to([DH, SEQ, LEN]))\
                .then_inc(v_small, 1)
            dve.tensor_copy(wg_T[0:DH, 0:C_EXP], bank(7)[0:DH, 64 + SEQ:64 + SEQ + C_EXP]).then_inc(v_small, 1)
            for s in range(HALVES):
                dve.wait_ge(pe_xT, s + 1)
                turned(s, bank(4 + s), 0)
            def c_unit(u):
                s, b = divmod(u, C_BLK)
                dve.wait_ge(act_g, u + 1)
                if u >= 2:
                    dve.wait_ge(v_hid, u - 1)
                link(dve.scalar_tensor_tensor(g_lk[:, u % 2], g_sb[:, u % 2], 0.01, g_sb[:, u % 2], ALU.mult, ALU.max))
                dve.tensor_tensor(c_hid[:, b, s * HW:(s + 1) * HW], g_lk[:, u % 2], bank(2 * (u % 2) + 1), ALU.mult)\
                    .then_inc(v_hid, 1)

            z, e8 = r_z[:, :, 0:8], r_s[:, :, 0:8]

            def bc(x, n=8):
                return x.unsqueeze(2).broadcast_to([P, TILES, n])

            def rank8(v):
                big = r_big[:, :].rearrange("p (t e f) -> p t e f", e=8, f=8)
                link(dve.tensor_tensor(big, v.unsqueeze(2).broadcast_to([P, TILES, 8, 8]),
                                       v.unsqueeze(3).broadcast_to([P, TILES, 8, 8]), ALU.subtract))
                link(dve.tensor_tensor(big, big, ahead8[:, :, :].unsqueeze(1).broadcast_to([P, TILES, 8, 8]),
                                       ALU.is_ge))
                link(dve.tensor_reduce(r_rank[:, :, 0:8], big, AX, ALU.add))

            dve.wait_ge(pe_log, 1)
            link(dve.tensor_scalar(z, bank(6)[:, 0:64].rearrange("p (t e) -> p t e", e=8), 0.5, None, ALU.mult))
            link(dve.tensor_reduce(r_sum[:, :], z, AX, ALU.max))
            dve.tensor_tensor(z, z, bc(r_sum[:, :]), ALU.subtract).then_inc(v_z, 1)
            c_unit(0)
            dve.wait_ge(act_exp, 1)
            link(dve.tensor_reduce(r_sum[:, :], e8, AX, ALU.add))
            link(dve.reciprocal(r_inv[:, :], r_sum[:, :]))
            link(dve.tensor_tensor(e8, e8, bc(r_inv[:, :]), ALU.mult))
            c_unit(1)
            dve.wait_ge(ready, 6)
            rank8(e8)
            c_unit(2)
            link(dve.scalar_tensor_tensor(z, r_rank[:, :, 0:8], 1.5, e8, ALU.is_lt, ALU.mult))
            link(dve.tensor_reduce(r_sum[:, :], z, AX, ALU.add))
            link(dve.tensor_scalar(r_sum[:, :], r_sum[:, :], 1e-20, None, ALU.add))
            link(dve.reciprocal(r_inv[:, :], r_sum[:, :]))
            dve.tensor_tensor(comb[:, 0:64].rearrange("p (e t) -> p t e", t=TILES), z, bc(r_inv[:, :]), ALU.mult)\
                .then_inc(v_comb, 1)
            c_unit(3)

            def rp_norm(n, sig):
                dve.wait_ge(act_rp, sig)
                link(dve.reciprocal(rp_sd[:, n:n + 1], rp_sd[:, n:n + 1]))
                link(dve.tensor_scalar(rp_h[:, 0, :], rp_h[:, 0, :], rp_mv[:, n, 0:1], rp_sd[:, n:n + 1],
                                       ALU.subtract, ALU.mult))
                dve.tensor_tensor(rp_h[:, 0, :], rp_h[:, 0, :], rp_rows[:, 2 + 2 * n, :], ALU.mult).then_inc(v_rp, 1)

            dve.wait_ge(ld["rp"], 128)
            dve.tensor_copy(iota16[:, :], iota_i[:, :])
            link(dve.tensor_copy(pos[:, :], pos_i[:, :]))
            link(dve.scalar_tensor_tensor(rp_h[:, 0, :], rp_rows[:, 0, :], pos[:, 0:1], rp_rows[:, 1, :],
                                          ALU.mult, ALU.add))
            link(dve.bn_stats(rp_st[:, :], rp_h[:, 0, :]))
            dve.bn_aggr(rp_mv[:, 0, :], rp_st[:, :]).then_inc(v_rp, 1)
            c_unit(4)
            c_unit(5)
            c_unit(6)
            dve.wait_ge(pe_small, 2)
            dve.tensor_copy(vec[:, :], bank(7)[:, 128:128 + V_ROWS]).then_inc(v_small, 1)
            dve.wait_ge(pe_comb, 1)
            dve.tensor_copy(comb_T[0:64, :], bank(5)[0:64, 0:P]).then_inc(v_combT, 1)
            c_unit(7)
            rp_norm(0, 1)
            c_unit(8)
            c_unit(9)
            for s in range(HALVES):
                dve.wait_ge(ld[f"gate_c{s}"], 32)
                cols = slice(s * HW, (s + 1) * HW)
                for q in range(3):
                    dve.wait_ge(v_hid, C_BLK * s + q + 1)
                    ins = dve.tensor_tensor(c_hid[:, q, cols], c_hid[:, q, cols], c_gate[:, q, cols], ALU.mult)
                ins.then_inc(v_mul, 1)
            for s in range(HALVES):
                dve.wait_ge(pe_down, s + 1)
                turned(s, bank(6 + s), 2)

            def f_unit(u):
                s, b = divmod(u, F_BLK)
                n = 2 * C_BLK + u
                dve.wait_ge(act_g, n + 1)
                dve.tensor_tensor(f_hid[:, b, s * HW:(s + 1) * HW], g_sb[:, n % 2], bank(2 * (n % 2) + 1), ALU.mult)\
                    .then_inc(v_hid, 1)

            f_unit(0)
            f_unit(1)
            dve.wait_ge(act_exp, 2)
            dve.wait_ge(ld["gk"], 64)
            link(dve.tensor_tensor(r_s[:, :, :], r_s[:, :, :], f_bias[:, :].unsqueeze(1).broadcast_to([P, TILES, 16]),
                                   ALU.add))
            g4 = r_s[:, :, :].rearrange("p t (g k) -> p t g k", k=4)
            ma, mb, lo_a, lo_b = r_a[:, :, :], r_b[:, :, :], r_c[:, :, :], r_d[:, :, :]
            dve.tensor_tensor(ma, g4[:, :, :, 0], g4[:, :, :, 1], ALU.max)
            dve.tensor_tensor(mb, g4[:, :, :, 2], g4[:, :, :, 3], ALU.max)
            dve.tensor_tensor(lo_a, g4[:, :, :, 0], g4[:, :, :, 1], ALU.min)
            link(dve.tensor_tensor(lo_b, g4[:, :, :, 2], g4[:, :, :, 3], ALU.min))
            link(dve.tensor_tensor(lo_a, lo_a, lo_b, ALU.max))
            link(dve.tensor_tensor(lo_b, ma, mb, ALU.min))
            link(dve.tensor_tensor(lo_a, lo_a, lo_b, ALU.max))
            link(dve.tensor_tensor(ma, ma, mb, ALU.max))
            link(dve.tensor_tensor(ma, ma, lo_a, ALU.add))
            f_unit(2)
            dve.wait_ge(pe_rp, 1)
            dve.tensor_copy(rp_T[:, 0, :], bank(7)[:, 256:256 + POSN]).then_inc(v_rp, 1)
            big4 = r_big[:, 0:P].rearrange("p (t e f) -> p t e f", e=4, f=4)
            link(dve.tensor_tensor(big4, ma.unsqueeze(2).broadcast_to([P, TILES, 4, 4]),
                                   ma.unsqueeze(3).broadcast_to([P, TILES, 4, 4]), ALU.subtract))
            link(dve.tensor_tensor(big4, big4, ahead4[:, :, :].unsqueeze(1).broadcast_to([P, TILES, 4, 4]), ALU.is_ge))
            link(dve.tensor_reduce(mb, big4, AX, ALU.add))
            link(dve.tensor_scalar(mb, mb, 1.5, None, ALU.is_lt))
            f_unit(3)
            link(dve.tensor_tensor(r_z[:, :, :].rearrange("p t (g k) -> p t g k", k=4), g4,
                                   mb.unsqueeze(3).broadcast_to([P, TILES, 4, 4]), ALU.mult))
            for t in range(TILES):
                dve.max(r_max[:, t, :], r_z[:, t, :])
            f_unit(4)
            dve.wait_ge(pe_rp, 2)
            link(dve.tensor_tensor(rp_h[:, 0, :], bank(7)[0:POSN, 320:448], rp_rows[:, 3, :], ALU.add))
            link(dve.bn_stats(rp_st[:, :], rp_h[:, 0, :]))
            dve.bn_aggr(rp_mv[:, 1, :], rp_st[:, :]).then_inc(v_rp, 1)
            for t in range(TILES):
                ins = dve.max_index(r_idx[:, t, :], r_max[:, t, :], r_z[:, t, :])
            link(ins)
            f_unit(5)
            link(dve.tensor_copy(r_idf[:, :, :], r_idx[:, :, :]))
            bigk = r_big[:, :].rearrange("p (t e k) -> p t e k", e=16, k=4)
            link(dve.tensor_tensor(bigk, r_idf[:, :, 0:4].unsqueeze(2).broadcast_to([P, TILES, 16, 4]),
                                   iota16[:, :].unsqueeze(1).unsqueeze(3).broadcast_to([P, TILES, 16, 4]),
                                   ALU.is_equal))
            link(dve.tensor_reduce(r_m[:, :, :], bigk, AX, ALU.add))
            f_unit(6)
            link(dve.tensor_tensor(r_z[:, :, :], r_z[:, :, :], r_m[:, :, :], ALU.mult))
            link(dve.tensor_reduce(r_sum[:, :], r_z[:, :, :], AX, ALU.add))
            link(dve.tensor_scalar(r_sum[:, :], r_sum[:, :], 1e-20, None, ALU.add))
            link(dve.reciprocal(r_inv[:, :], r_sum[:, :]))
            link(dve.tensor_tensor(r_z[:, :, :], r_z[:, :, :], bc(r_inv[:, :], 16), ALU.mult))
            dve.tensor_scalar(comb[:, :].rearrange("p (e t) -> p t e", t=TILES), r_z[:, :, :], F_SCALE, None, ALU.mult)\
                .then_inc(v_comb, 1)
            f_unit(7)
            rp_norm(1, 3)
            for u in range(8, 16):
                f_unit(u)
                if u == 10:
                    dve.wait_ge(pe_rp, 3)
                    dve.tensor_copy(rp_T[:, 1, :], bank(7)[:, 256:256 + POSN]).then_inc(v_rp, 1)
                if u == 13:
                    dve.wait_ge(pe_rp, 4)
                    dve.tensor_scalar(rp_out[:, :], bank(7)[0:HEADS, 320:320 + POSN], rp_b2[:, 0:1], None, ALU.add)\
                        .then_inc(v_rp, 2)
                if u == 11:
                    dve.wait_ge(pe_comb, 2)
                    dve.tensor_copy(comb_T[:, :], bank(5)[:, 0:P]).then_inc(v_combT, 1)
            f_unit(16)
            f_unit(17)
            for s in range(HALVES):
                cols = slice(s * HW, (s + 1) * HW)
                dve.wait_ge(ld[f"gate_f{s}"], 32)
                for q in range(5):
                    dve.wait_ge(v_hid, 2 * C_BLK + F_BLK * s + q + 1)
                    ins = dve.tensor_tensor(f_hid[:, q, cols], f_hid[:, q, cols], f_gate[:, q, cols], ALU.mult)
                ins.then_inc(v_mul, 1)
            def norm_stats(s):
                dve.wait_ge(pe_down, 2 + s + 1)
                xs = x_tok[:, s * HT:(s + 1) * HT, :].rearrange("p t c -> p (t c)")
                link(dve.tensor_tensor(xs, xs, bank(6 + s), ALU.add))
                for t in range(HT):
                    ins = dve.bn_stats(st6[:, s, t, :], x_tok[:, s * HT + t, :])
                link(ins)
                for t in range(HT):
                    ins = dve.bn_aggr(mv[:, s * HT + t, :], st6[:, s, t, :])
                ins.then_inc(v_var, 1)

            def normed(s):
                dve.wait_ge(pool_rstd, s + 1)
                for t in range(s * HT, (s + 1) * HT):
                    ins = dve.tensor_scalar(xn_tok[:, t, :], x_tok[:, t, :], mv[:, t, 0:1], rstd[:, t:t + 1],
                                            ALU.subtract, ALU.mult)
                ins.then_inc(v_xn, 1)

            dve.wait_ge(ld["att"], 160)
            dve.wait_ge(ready, 11)
            for h in range(2):
                rows = slice(h * DH, (h + 1) * DH)
                dst = nv_sel[rows, :, :].rearrange("p b h -> p (b h)")[:, h:h + 18 * 7 + 1:18]
                ins = dve.tensor_copy(dst, nv_col[rows, 0:1].broadcast_to([DH, HB]))
            ins.then_inc(v_nv, 1)
            link(dve.tensor_tensor(s_dup[:, :], qk_scale[:, 0, :], qk_scale[:, 1, :], ALU.mult))
            link(dve.tensor_scalar(s_dup[:, :], s_dup[:, :], ATT_SCALE, None, ALU.mult))
            link(dve.tensor_scalar(mask_add[:, :, :], mask_u8[:, :, :], 1.0, -MASKED, ALU.subtract, ALU.mult))
            norm_stats(0)
            dve.tensor_copy(att_bias[:, :, :, LEN], null_b[:, :].unsqueeze(1).broadcast_to([P, TILES, HEADS]))
            normed(0)
            dve.wait_ge(pool_bias, BPT)

            def biases(tiles):
                for t in tiles:
                    ins = dve.tensor_tensor(att_bias[:, t, :, 0:LEN], base_bias[:, :, :],
                                            mask_add[:, t, :].unsqueeze(1).broadcast_to([P, HEADS, LEN]), ALU.add)
                ins.then_inc(v_bias, 1)

            biases(range(0, 5))
            norm_stats(1)
            dve.wait_ge(pe_xT, 3)
            dve.wait_ge(v_small, 4)
            turned(0, bank(4), 4, scale=vec[:, V_GN:V_GN + 1])
            normed(1)
            dve.wait_ge(pe_nv, 1)
            dve.tensor_copy(nv_out[0:HEADS, :], bank(3)[0:HEADS, 0:P]).then_inc(v_nvo, 1)
            dve.wait_ge(pe_xT, 4)
            turned(1, bank(5), 4, scale=vec[:, V_GN:V_GN + 1])

            def keys_and_values(s):
                dve.wait_ge(pe_kv, s + 1)
                kv = bank(6 + s).rearrange("p (t c) -> p t c", c=P)
                dve.tensor_copy(k_tok[:, s * HT:(s + 1) * HT, :], kv[:, :, 0:DH])
                for q in range(BPT):
                    rows = slice(q * LEN, (q + 1) * LEN)
                    ins = dve.tensor_copy(v_diag[rows, s * HT:(s + 1) * HT, q, :], kv[rows, :, DH:P])
                if s == 1:
                    ins.then_inc(v_kv, 1)

            def q_norm(t):
                dve.wait_ge(act_sq, t + 1)
                dve.tensor_reduce(n2[:, t, :], q_sq[:, t % 2, :].rearrange("p (h d) -> p h d", d=DH), AX, ALU.add)\
                    .then_inc(v_red, 1)
                dve.wait_ge(act_sqrt, 1 + t + (t > 2))
                link(dve.tensor_scalar(rn[:, t, :], rn[:, t, :], NORM_EPS, None, ALU.max))
                link(dve.reciprocal(rn[:, t, :], rn[:, t, :]))
                if t >= 2:
                    dve.wait_ge(pe_qT, t - 1)
                dve.tensor_tensor(q_hat[:, t % 2, :].rearrange("p (h d) -> p h d", d=DH),
                                  ps[:, 2 * (t % 2):2 * (t % 2) + 2, :].rearrange("p b (h d) -> p (b h) d", d=DH),
                                  rn[:, t, :].unsqueeze(2).broadcast_to([P, HEADS, DH]), ALU.mult)\
                    .then_inc(v_qhat, 1)

            q_norm(0)
            keys_and_values(0)
            keys_and_values(1)
            q_norm(1)
            dve.wait_ge(v_kv, 1)
            dve.wait_ge(ld["null"], 16)
            link(dve.tensor_tensor(k_sq, k_tok, k_tok, ALU.mult))
            dve.tensor_reduce(k2sum[:, :], k_sq, AX, ALU.add).then_inc(v_n2, 1)
            q_norm(2)
            q_norm(3)
            dve.wait_ge(act_sqrt, 4)
            link(dve.tensor_scalar(k2rn[:, :], k2rn[:, :], NORM_EPS, None, ALU.max))
            link(dve.reciprocal(k2rn[:, :], k2rn[:, :]))
            link(dve.tensor_tensor(k_tok, k_tok, k2rn[:, :].unsqueeze(2).broadcast_to([P, TILES + 1, DH]), ALU.mult))
            for h in range(2):
                ins = dve.tensor_tensor(k_dup[:, :, h, :], k_tok,
                                        s_dup[:, :].unsqueeze(1).broadcast_to([P, TILES + 1, DH]), ALU.mult)
            ins.then_inc(v_k, 1)
            for t in range(4, TILES):
                q_norm(t)
            biases(range(5, TILES))
            dve.wait_ge(pe_kT, 1)
            for h in range(2):
                rows = slice(h * DH, (h + 1) * DH)
                for s in range(HALVES):
                    dve.tensor_copy(k_diag[rows, s * HT * BPT:(s + 1) * HT * BPT, h, 0:LEN],
                                    bank(s)[rows, :].rearrange("p (b k) -> p b k", k=LEN))
                ins = dve.tensor_copy(k_diag[rows, :, h, LEN], bank(2)[rows, 0:SEQ])
            ins.then_inc(v_kd, 1)

            def scored(t):
                dve.wait_ge(pe_sim, t + 1)
                if t >= 2:
                    dve.wait_ge(act_pexp, t - 1)
                if t == 0:
                    dve.wait_ge(pe_qT, TILES)
                link(dve.tensor_tensor(s_buf[:, t % 2].rearrange("p (g h) k -> p g (h k)", g=2),
                                       ps[:, 2 * (t % 2):2 * (t % 2) + 2, 0:8 * KEYS],
                                       att_bias[:, t].rearrange("p (g h) k -> p g (h k)", g=2), ALU.add))
                dve.tensor_reduce(smax[:, t % 2, :], s_buf[:, t % 2], AX, ALU.max).then_inc(v_max, 1)

            def summed(t):
                dve.wait_ge(act_pexp, t + 1)
                if t >= 2:
                    dve.wait_ge(pool_prob, t - 1)
                link(dve.tensor_reduce(ssum[:, t % 2, :], e_buf[:, t % 2], AX, ALU.add))
                dve.reciprocal(ssum[:, t % 2, :], ssum[:, t % 2, :]).then_inc(v_rs, 1)
                dve.wait_ge(v_rs, t + 1)
                if t >= 2:
                    dve.wait_ge(pe_pn, t - 1)
                dve.tensor_tensor(p_null[:, t % 2, :], e_buf[:, t % 2, :, LEN], ssum[:, t % 2, :], ALU.mult)\
                    .then_inc(v_pn, 1)

            def turned_probs(t):
                dve.wait_ge(pool_prob, t + 1)
                if t >= 2:
                    dve.wait_ge(pe_av, t - 1)
                dve.transpose(pT_buf[:, t % 2].rearrange("p h k -> p (h k)"),
                              p_buf[:, t % 2].rearrange("p h k -> p (h k)")).then_inc(v_pT, 1)

            def projected(t):
                dve.wait_ge(pe_wo, t + 1)
                link(dve.bn_stats(st6[:, 0, 0, :], bank(6)[:, 0:P]))
                dve.bn_aggr(mv[:, t, :], st6[:, 0, 0, :]).then_inc(v_st, 1)

            def att_normed(t):
                dve.wait_ge(pool_rstd, 2 + 2 * t + 1)
                dve.tensor_scalar(xc[:, t, :], bank(6)[:, 0:P], mv[:, t, 0:1], rstd[:, t:t + 1],
                                  ALU.subtract, ALU.mult).then_inc(v_wo, 1)
                dve.wait_ge(v_wo, t + 1)
                dve.tensor_tensor(xc[:, t, :], xc[:, t, :], g_out[:, :], ALU.mult).then_inc(v_xc, 1)
                dve.wait_ge(v_xc, t + 1)
                link(dve.bn_stats(st6[:, 0, 1, :], xc[:, t, :]))
                dve.bn_aggr(mv[:, t, :], st6[:, 0, 1, :]).then_inc(v_st2, 1)

            def input_normed(t):
                dve.wait_ge(pool_rstd, 2 + 2 * t + 2)
                if t >= 2:
                    dve.wait_ge(pe_xcT, t - 1)
                dve.tensor_scalar(xh_tok[:, t % 2, :], xc[:, t, :], mv[:, t, 0:1], rstd[:, t:t + 1],
                                  ALU.subtract, ALU.mult).then_inc(v_xh, 1)

            scored(0)
            scored(1)
            summed(0)
            turned_probs(0)
            for t in range(TILES):
                if t + 1 < TILES:
                    summed(t + 1)
                if t >= 1:
                    projected(t - 1)
                if t + 1 < TILES:
                    turned_probs(t + 1)
                if t >= 1:
                    att_normed(t - 1)
                if t + 2 < TILES:
                    scored(t + 2)
                if t >= 1:
                    input_normed(t - 1)
            projected(TILES - 1)
            att_normed(TILES - 1)
            input_normed(TILES - 1)
            steps = M_EXP * HALVES

            def split_gelu(k, half):
                b = slice(2 * half, 2 * half + 2)
                dve.wait_ge(act_gelu, M_BLK * k + 2 * half + 2)
                if k >= 2:
                    dve.wait_ge(pe_m_down, k - 1)
                if half == 0:
                    dve.tensor_copy(g_hi[:, k % 2, b, :], gelu[:, k % 2, b, :]).then_inc(v_ghi, 1)
                    dve.wait_ge(v_ghi, k + 1)
                else:
                    dve.wait_ge(act_ghi, k + 1)
                dve.tensor_tensor(g_lo[:, k % 2, b, :], gelu[:, k % 2, b, :], g_hi[:, k % 2, b, :].bitcast(f32),
                                  ALU.subtract).then_inc(v_glo, 1)

            split_gelu(0, 0)
            split_gelu(0, 1)
            dve.wait_ge(pe_log, 2 + TILES)
            link(dve.tensor_tensor(z, bank(7)[:, 256:320].rearrange("p (t e) -> p t e", e=8),
                                   router_b[:, :].unsqueeze(1).broadcast_to([P, TILES, 8]), ALU.add))
            rank8(z)
            link(dve.tensor_reduce(r_sum[:, :], z, AX, ALU.max))
            dve.tensor_tensor(z, z, bc(r_sum[:, :]), ALU.subtract).then_inc(v_z, 1)
            dve.wait_ge(act_exp, 3)
            link(dve.scalar_tensor_tensor(z, r_rank[:, :, 0:8], 1.5, e8, ALU.is_lt, ALU.mult))
            link(dve.tensor_reduce(r_sum[:, :], z, AX, ALU.add))
            link(dve.reciprocal(r_inv[:, :], r_sum[:, :]))
            link(dve.tensor_tensor(z, z, bc(r_inv[:, :]), ALU.mult))
            dve.tensor_copy(comb[:, 0:64].rearrange("p (e t) -> p t e", t=TILES), z).then_inc(v_comb, 1)
            split_gelu(1, 0)
            split_gelu(1, 1)
            link(dve.tensor_reduce(g_sum[:, :], z, AX, ALU.add))
            dve.wait_ge(pe_comb, 3)
            dve.tensor_copy(comb_T[0:64, :], bank(5)[0:64, 0:P]).then_inc(v_combT, 1)
            for t in range(TILES):
                ins = dve.scalar_tensor_tensor(x_tok[:, t, :], xc[:, t, :], g_sum[:, t:t + 1], x_tok[:, t, :],
                                               ALU.mult, ALU.add)
            link(ins)
            for k in range(steps):
                e, s = divmod(k, HALVES)
                dve.wait_ge(pe_m_down, k + 1)
                dve.wait_ge(m_gate_in[e], 16)
                if k >= 2:
                    dve.wait_ge(pool_acc, k - 1)
                dve.scalar_tensor_tensor(y_tmp[:, k % 2], bank(6 + k % 2), vec[:, V_B2 + e:V_B2 + e + 1],
                                         m_gate[:, e, s * HW:(s + 1) * HW], ALU.add, ALU.mult).then_inc(v_y, 1)
                if k + 2 < steps:
                    split_gelu(k + 2, 0)
                    split_gelu(k + 2, 1)
            for s in range(HALVES):
                dve.wait_ge(pe_fin, s + 1)
                xs = x_tok[:, s * HT:(s + 1) * HT, :].rearrange("p t c -> p (t c)")
                dve.tensor_tensor(xs, xs, bank(4 + s), ALU.add).then_inc(v_out, 1)


_INS = ['x', 'cond_64', 'mask_BxS_bf1', 'L0_cond_wt', 'L0_cond_wg', 'L0_cond_w_gate', 'L0_cond_w_up',
        'L0_cond_w_down', 'L0_cond_sw_gate', 'L0_cond_sw_up', 'L0_cond_sw_down', 'L0_ffn_gate_kernel',
        'L0_ffn_gate_bias', 'L0_ffn_w_gate', 'L0_ffn_w_up', 'L0_ffn_w_down', 'L0_ffn_sw_gate', 'L0_ffn_sw_up',
        'L0_ffn_sw_down', 'L1_cond_g_norm', 'L1_cond_Wq', 'L1_cond_Wkv', 'L1_cond_q_scale', 'L1_cond_k_scale',
        'L1_cond_null_attn_bias', 'L1_cond_w0', 'L1_cond_b0', 'L1_cond_g0', 'L1_cond_w1', 'L1_cond_b1',
        'L1_cond_g1', 'L1_cond_w2', 'L1_cond_b2', 'L1_cond_Wout', 'L1_cond_g_out', 'L1_ffn_router_W',
        'L1_ffn_router_b', 'L1_ffn_ln_g', 'L1_ffn_ln_b', 'L1_ffn_W1', 'L1_ffn_b1', 'L1_ffn_W2', 'L1_ffn_b2']


def kernel(**inputs):
    import numpy as _np
    import concourse.bacc as _bacc
    from concourse import mybir as _mybir
    from concourse.bass_utils import run_bass_kernel_spmd as _run

    nc = _bacc.Bacc("TRN2", target_bir_lowering=False, num_devices=1)
    arrays, views = {}, {}
    for name in _INS:
        v = _np.ascontiguousarray(inputs[name])
        if v.dtype == _np.bool_:
            v = v.view(_np.uint8)
        arrays[f"in_{name}"] = v
        views[name] = nc.dram_tensor(f"in_{name}", v.shape, _mybir.dt.from_np(v.dtype), kind="ExternalInput").ap()
    out = nc.dram_tensor("out_0", (SEQ, LEN, P), f32, kind="ExternalOutput").ap()
    two_layers(nc, views, out)
    r = _run(nc, [arrays], core_ids=[0])
    return r.results[0]["out_0"]
```
